# Optimizing a Trainium2 kernel written in Bass

```python
import numpy as np
import jax
import jax.numpy as jnp

def _softmax(x, axis=-1):
    return jax.nn.softmax(x, axis=axis)

def _gelu(x):
    return jax.nn.gelu(x, approximate=True)

def _silu(x):
    return jax.nn.silu(x)

def _sigmoid(x):
    return jax.nn.sigmoid(x)

def _layernorm(x, axis=-1, eps=1e-05):
    m = jnp.mean(x, axis=axis, keepdims=True)
    v = jnp.var(x, axis=axis, keepdims=True)
    return (x - m) / jnp.sqrt(v + eps)

def _scatter_add(tgt, idx, src, axis=0):
    return tgt.at[idx].add(src)

def _segment_sum(src, seg, n):
    return jax.ops.segment_sum(src, seg, n)
kernel_name = 'mk_vit_tower_d2_tok_img512_r4_bbe458'

def setup_inputs(seed: int=0):
    np.random.seed(seed)
    _w = jnp.asarray

    def _rec_inputs():
        import jax
        import jax.numpy as jnp
        _rk = jax.random.key(seed)
        x = -0.000147625 + 0.999875 * jax.random.normal(jax.random.fold_in(_rk, 1), (128, 3, 224, 224), jnp.float32)
        return x
    x = _rec_inputs()

    def _L0_tok_setup():
        import jax, jax.numpy as jnp
        import numpy as np
        N_PATCHES = 8
        PATCH = 28
        C = 3
        IN_D = C * PATCH * PATCH
        HID = 128
        SEQ = N_PATCHES * N_PATCHES + 1

        def _positional_embedding(seq_len, dim):
            i = np.arange(seq_len)[:, None].astype(np.float32)
            j = np.arange(dim)[None, :].astype(np.float32)
            ang = i / np.power(100000.0, j / dim)
            pe = np.where(j % 2 == 0, np.sin(ang), np.cos(ang))
            return jnp.asarray(pe, dtype=jnp.float32)
        key = jax.random.key(seed)
        k1, k2, k3, k4 = jax.random.split(key, 4)
        B = 64
        X = jax.random.normal(k1, (B, C, 224, 224), dtype=jnp.float32)
        bound = 1.0 / np.sqrt(IN_D)
        W = jax.random.uniform(k2, (HID, IN_D), minval=-bound, maxval=bound, dtype=jnp.float32)
        b = jax.random.uniform(k3, (HID,), minval=-bound, maxval=bound, dtype=jnp.float32)
        class_token = jax.random.uniform(k4, (1, HID), dtype=jnp.float32)
        pos_embed = _positional_embedding(SEQ, HID)
        return {'X': X, 'W': W, 'b': b, 'class_token': class_token, 'pos_embed': pos_embed}
    _L0_tok_all = _L0_tok_setup()
    _L0_tok_in = {k: v for k, v in _L0_tok_all.items() if k in ('W', 'b', 'class_token', 'pos_embed')}
    del _L0_tok_all

    def _L0_attn_setup():
        import jax, jax.numpy as jnp
        import numpy as np
        B, N, DIM = (4, 512, 128)
        H, DH, ORDER, TOPK = (8, 64, 3, 64)
        INNER = H * DH
        SCALE = DH ** (-0.5)
        key = jax.random.key(seed)
        ks = jax.random.split(key, 6)
        x = jax.random.normal(ks[0], (B, N, DIM), dtype=jnp.float32)
        Wqkv = jax.random.normal(ks[1], (DIM, 3 * INNER), dtype=jnp.float32) * DIM ** (-0.5)
        bqkv = jax.random.normal(ks[2], (3 * INNER,), dtype=jnp.float32) * 0.01
        Wout = jax.random.normal(ks[3], (INNER, DIM), dtype=jnp.float32) * INNER ** (-0.5)
        bout = jax.random.normal(ks[4], (DIM,), dtype=jnp.float32) * 0.01
        alphas_raw = jnp.ones((ORDER, H), dtype=jnp.float32) / ORDER
        return {'x': x, 'Wqkv': Wqkv, 'bqkv': bqkv, 'Wout': Wout, 'bout': bout, 'alphas_raw': alphas_raw}
    _L0_attn_all = _L0_attn_setup()
    _L0_attn_in = {k: v for k, v in _L0_attn_all.items() if k in ('Wqkv', 'bqkv', 'Wout', 'bout', 'alphas_raw')}
    del _L0_attn_all

    def _L0_ffn_setup():
        import jax, jax.numpy as jnp
        import numpy as np
        E = 64
        K = 2
        CAP = 128
        H = 128
        FFN = 512
        B, S = (8, 1024)
        key = jax.random.key(seed)
        ks = jax.random.split(key, 6)
        hidden_states = jax.random.normal(ks[0], (B, S, H), dtype=jnp.float32)
        router_w = jax.random.normal(ks[1], (E, H), dtype=jnp.float32) * (0.01 / np.sqrt(H))
        w1 = jax.random.normal(ks[2], (FFN, H), dtype=jnp.float32) * (1.0 / np.sqrt(H))
        b1 = jnp.zeros((FFN,), dtype=jnp.float32)
        w2 = jax.random.normal(ks[3], (H, FFN), dtype=jnp.float32) * (1.0 / np.sqrt(FFN))
        b2 = jnp.zeros((H,), dtype=jnp.float32)
        return {'hidden_states': hidden_states, 'router_w': router_w, 'w1': w1, 'b1': b1, 'w2': w2, 'b2': b2}
    _L0_ffn_all = _L0_ffn_setup()
    _L0_ffn_in = {k: v for k, v in _L0_ffn_all.items() if k in ('router_w', 'w1', 'b1', 'w2', 'b2')}
    del _L0_ffn_all

    def _L1_attn_setup():
        import jax, jax.numpy as jnp
        import numpy as np
        import math
        HEADS = 8
        DIM_HEAD = 64
        key = jax.random.key(seed)
        k1, k2, k3 = jax.random.split(key, 3)
        b, n, dim = (4, 512, 128)
        inner = HEADS * DIM_HEAD
        x = jax.random.normal(k1, (b, n, dim), dtype=jnp.float32)
        W_qkv = jax.random.normal(k2, (dim, 4 * inner), dtype=jnp.float32) * dim ** (-0.5)
        W_out = jax.random.normal(k3, (2 * inner, dim), dtype=jnp.float32) * (2 * inner) ** (-0.5)
        b_out = jnp.zeros((dim,), dtype=jnp.float32)
        return {'x': x, 'W_qkv': W_qkv, 'W_out': W_out, 'b_out': b_out}
    _L1_attn_all = _L1_attn_setup()
    _L1_attn_in = {k: v for k, v in _L1_attn_all.items() if k in ('W_qkv', 'W_out', 'b_out')}
    del _L1_attn_all

    def _L1_ffn_setup():
        import jax, jax.numpy as jnp
        import numpy as np
        B, S, H, E, K = (8, 1024, 128, 8, 2)
        key = jax.random.key(seed)
        ks = jax.random.split(key, 7)
        s_h = 1.0 / np.sqrt(H)
        s_2h = 1.0 / np.sqrt(2 * H)
        return {'x': jax.random.normal(ks[0], (B, S, H), dtype=jnp.float32), 'gate_w': jax.random.uniform(ks[1], (H, E), minval=-s_h, maxval=s_h, dtype=jnp.float32), 'gate_b': jax.random.uniform(ks[2], (E,), minval=-s_h, maxval=s_h, dtype=jnp.float32), 'w1': jax.random.uniform(ks[3], (E, H, 2 * H), minval=-s_h, maxval=s_h, dtype=jnp.float32), 'b1': jax.random.uniform(ks[4], (E, 2 * H), minval=-s_h, maxval=s_h, dtype=jnp.float32), 'w2': jax.random.uniform(ks[5], (E, 2 * H, H), minval=-s_2h, maxval=s_2h, dtype=jnp.float32), 'b2': jax.random.uniform(ks[6], (E, H), minval=-s_2h, maxval=s_2h, dtype=jnp.float32)}
    _L1_ffn_all = _L1_ffn_setup()
    _L1_ffn_in = {k: v for k, v in _L1_ffn_all.items() if k in ('gate_w', 'gate_b', 'w1', 'b1', 'w2', 'b2')}
    del _L1_ffn_all
    return {'x': x, 'L0_tok_W': _L0_tok_in['W'], 'L0_tok_b': _L0_tok_in['b'], 'L0_tok_class_token': _L0_tok_in['class_token'], 'L0_tok_pos_embed': _L0_tok_in['pos_embed'], 'L0_attn_Wqkv': _L0_attn_in['Wqkv'], 'L0_attn_bqkv': _L0_attn_in['bqkv'], 'L0_attn_Wout': _L0_attn_in['Wout'], 'L0_attn_bout': _L0_attn_in['bout'], 'L0_attn_alphas_raw': _L0_attn_in['alphas_raw'], 'L0_ffn_router_w': _L0_ffn_in['router_w'], 'L0_ffn_w1': _L0_ffn_in['w1'], 'L0_ffn_b1': _L0_ffn_in['b1'], 'L0_ffn_w2': _L0_ffn_in['w2'], 'L0_ffn_b2': _L0_ffn_in['b2'], 'L1_attn_W_qkv': _L1_attn_in['W_qkv'], 'L1_attn_W_out': _L1_attn_in['W_out'], 'L1_attn_b_out': _L1_attn_in['b_out'], 'L1_ffn_gate_w': _L1_ffn_in['gate_w'], 'L1_ffn_gate_b': _L1_ffn_in['gate_b'], 'L1_ffn_w1': _L1_ffn_in['w1'], 'L1_ffn_b1': _L1_ffn_in['b1'], 'L1_ffn_w2': _L1_ffn_in['w2'], 'L1_ffn_b2': _L1_ffn_in['b2']}

def reference(x, L0_tok_W, L0_tok_b, L0_tok_class_token, L0_tok_pos_embed, L0_attn_Wqkv, L0_attn_bqkv, L0_attn_Wout, L0_attn_bout, L0_attn_alphas_raw, L0_ffn_router_w, L0_ffn_w1, L0_ffn_b1, L0_ffn_w2, L0_ffn_b2, L1_attn_W_qkv, L1_attn_W_out, L1_attn_b_out, L1_ffn_gate_w, L1_ffn_gate_b, L1_ffn_w1, L1_ffn_b1, L1_ffn_w2, L1_ffn_b2):
    import jax
    import jax.numpy as jnp

    def _L0_tok_ref(X, W, b, class_token, pos_embed):
        import jax, jax.numpy as jnp
        import numpy as np
        N_PATCHES = 8
        PATCH = 28
        C = 3
        IN_D = C * PATCH * PATCH
        HID = 128
        SEQ = N_PATCHES * N_PATCHES + 1

        def _positional_embedding(seq_len, dim):
            i = np.arange(seq_len)[:, None].astype(np.float32)
            j = np.arange(dim)[None, :].astype(np.float32)
            ang = i / np.power(100000.0, j / dim)
            pe = np.where(j % 2 == 0, np.sin(ang), np.cos(ang))
            return jnp.asarray(pe, dtype=jnp.float32)
        B = X.shape[0]
        patches = X.reshape(B, C, N_PATCHES, PATCH, N_PATCHES, PATCH)
        patches = patches.transpose(0, 2, 4, 1, 3, 5).reshape(B, N_PATCHES * N_PATCHES, IN_D)
        tokens = jnp.einsum('bpi,hi->bph', patches, W) + b
        cls = jnp.broadcast_to(class_token[None, :, :], (B, 1, HID))
        tokens = jnp.concatenate([cls, tokens], axis=1)
        return tokens * pos_embed[None, :, :]

    def _L0_attn_ref(x, Wqkv, bqkv, Wout, bout, alphas_raw):
        import jax, jax.numpy as jnp
        import numpy as np
        B, N, DIM = (4, 512, 128)
        H, DH, ORDER, TOPK = (8, 64, 3, 64)
        INNER = H * DH
        SCALE = DH ** (-0.5)
        b, n, _ = x.shape
        qkv = x @ Wqkv + bqkv
        q, k, v = jnp.split(qkv, 3, axis=-1)
        to_heads = lambda t: t.reshape(b, n, H, DH).transpose(0, 2, 1, 3)
        q, k, v = (to_heads(q), to_heads(k), to_heads(v))
        scores = jnp.einsum('bhnd,bhmd->bhnm', q, k) * SCALE
        top_val = jax.lax.top_k(scores, TOPK)[0][..., -1:]
        scores = jnp.where(scores < top_val, -jnp.inf, scores)
        attn = jax.nn.softmax(scores, axis=-1)
        attn32 = attn.astype(jnp.float32)
        v_curr = v.astype(jnp.float32)
        alphas = jax.nn.gelu(alphas_raw.astype(jnp.float32), approximate=False)
        res = jnp.zeros_like(v_curr)
        for i in range(ORDER):
            v_curr = attn32 @ v_curr
            res = res + alphas[i].reshape(1, H, 1, 1) * v_curr
        out = res.astype(x.dtype).transpose(0, 2, 1, 3).reshape(b, n, INNER)
        return out @ Wout + bout

    def _L0_ffn_ref(hidden_states, router_w, w1, b1, w2, b2):
        import jax, jax.numpy as jnp
        import numpy as np
        E = 64
        K = 2
        CAP = 128
        H = 128
        FFN = 512
        B, S = (8, 1024)
        orig_shape = hidden_states.shape
        x = hidden_states.reshape(-1, orig_shape[-1])
        T = x.shape[0]
        N = T * K
        logits = jnp.einsum('th,eh->te', x, router_w)
        probs_full = jax.nn.softmax(logits, axis=-1)
        probs, idx = jax.lax.top_k(probs_full, K)
        flat_e = idx.reshape(-1)
        flat_p = probs.reshape(-1)
        order = jnp.argsort(flat_e, stable=True)
        sorted_e = flat_e[order]
        counts = jnp.zeros((E,), jnp.int32).at[flat_e].add(1)
        offsets = jnp.concatenate([jnp.zeros((1,), jnp.int32), jnp.cumsum(counts)[:-1]])
        pos = jnp.arange(N, dtype=jnp.int32) - offsets[sorted_e]
        keep = pos < CAP
        slot = sorted_e * CAP + jnp.minimum(pos, CAP - 1)
        dest = jnp.where(keep, slot, E * CAP)
        tok = order // K
        buf = jnp.zeros((E * CAP + 1, x.shape[-1]), x.dtype).at[dest].set(x[tok])
        buf = buf[:-1]
        h = jax.nn.gelu(jnp.einsum('nh,fh->nf', buf, w1) + b1, approximate=False)
        y = jnp.einsum('nf,hf->nh', h, w2) + b2
        gate = jnp.where(keep, flat_p[order], 0.0)
        contrib = y[jnp.minimum(slot, E * CAP - 1)] * gate[:, None]
        out = jnp.zeros_like(x).at[tok].add(contrib)
        return out.reshape(orig_shape)

    def _L1_attn_ref(x, W_qkv, W_out, b_out):
        import jax, jax.numpy as jnp
        import numpy as np
        import math
        HEADS = 8
        DIM_HEAD = 64
        b, n, d = x.shape
        h, dh = (HEADS, DIM_HEAD)
        scale = dh ** (-0.5)
        qkvt = x @ W_qkv
        q, k, v, t = jnp.split(qkvt, 4, axis=-1)

        def to_heads(z):
            return z.reshape(b, n, h, dh).transpose(0, 2, 1, 3)
        q, k, v, t = map(to_heads, (q, k, v, t))
        dots = jnp.einsum('bhid,bhjd->bhij', q, k) * scale
        attn1 = jax.nn.softmax(dots, axis=-1)
        out1 = jnp.einsum('bhij,bhjd->bhid', attn1, v)
        pos = jnp.arange(1, n + 1, dtype=x.dtype)
        tg = jnp.abs(pos[None, :] - pos[:, None])
        attn2 = jnp.exp(-tg / jnp.asarray(math.e, dtype=x.dtype))
        attn2 = attn2 / attn2.sum(-1)
        out2 = jnp.einsum('ij,bhjd->bhid', attn2, t)
        out = jnp.concatenate([out1, out2], axis=-1)
        out = out.transpose(0, 2, 1, 3).reshape(b, n, 2 * h * dh)
        return out @ W_out + b_out

    def _L1_ffn_ref(x, gate_w, gate_b, w1, b1, w2, b2):
        import jax, jax.numpy as jnp
        import numpy as np
        B, S, H, E, K = (8, 1024, 128, 8, 2)
        logits = jnp.einsum('bsh,he->bse', x, gate_w) + gate_b
        topk_vals, topk_idx = jax.lax.top_k(logits, K)
        topk_weights = jax.nn.softmax(topk_vals, axis=-1)
        mask = jax.nn.one_hot(topk_idx, E, dtype=topk_weights.dtype)
        weights = jnp.einsum('bske,bsk->bse', mask, topk_weights)
        h = jax.nn.relu(jnp.einsum('bsh,ehf->bsef', x, w1) + b1)
        expert_out = jnp.einsum('bsef,efh->bseh', h, w2) + b2
        return jnp.einsum('bseh,bse->bsh', expert_out, weights)
    h = _L0_tok_ref(x, L0_tok_W, L0_tok_b, L0_tok_class_token, L0_tok_pos_embed)
    h = h + _L0_attn_ref(_layernorm(h, axis=-1), L0_attn_Wqkv, L0_attn_bqkv, L0_attn_Wout, L0_attn_bout, L0_attn_alphas_raw)
    h = h + _L0_ffn_ref(_layernorm(h, axis=-1), L0_ffn_router_w, L0_ffn_w1, L0_ffn_b1, L0_ffn_w2, L0_ffn_b2)
    h = h + _L1_attn_ref(_layernorm(h, axis=-1), L1_attn_W_qkv, L1_attn_W_out, L1_attn_b_out)
    h = h + _L1_ffn_ref(_layernorm(h, axis=-1), L1_ffn_gate_w, L1_ffn_gate_b, L1_ffn_w1, L1_ffn_b1, L1_ffn_w2, L1_ffn_b2)
    return h

_drawn_inputs = setup_inputs


def setup_inputs(seed=0):
    import zlib

    import numpy as np

    out = dict(_drawn_inputs(seed))
    spreads = {'L0_attn_alphas_raw': (0.3333333432674408, 0.2),
     'L0_ffn_b1': (0.0, 0.422),
     'L0_ffn_b2': (0.0, 0.362),
     'L1_attn_b_out': (0.0, 0.1)}
    factors = {}
    for name, (base, spread) in spreads.items():
        noise = np.random.default_rng([zlib.crc32(name.encode()), seed]).standard_normal(out[name].shape)
        drawn = base * np.exp(spread * noise) if base else spread * noise
        out[name] = jnp.asarray(drawn.astype(out[name].dtype))
    for name, factor in factors.items():
        out[name] = (out[name] * factor).astype(out[name].dtype)
    return out
```

```python
import concourse.bass as bass
from concourse import mybir
from contextlib import ExitStack

FP32 = mybir.dt.float32
U32 = mybir.dt.uint32
BF16 = mybir.dt.bfloat16
ALU = mybir.AluOpType
ACT = mybir.ActivationFunctionType
AX = mybir.AxisListType

P = 128
D = 128
GRID = 8
PATCHES = GRID * GRID
SEQ = PATCHES + 1
PATCH = 28
IN_D = 3 * PATCH * PATCH
KT = IN_D // P
KR = IN_D - KT * P
H, DH = 8, 64
INNER = H * DH
CH = INNER // P
SCALE = DH ** -0.5
ORDER = 3
E0, E1 = 64, 8
CAPACITY = 128
F0, F1 = 512, 256
EPS = 1e-5
BANK = 512
CHUNK_IMAGES = 8


class At:

    def __init__(self, index, slot):
        self.index, self.slot = index, slot


def pipelined(eng, items, unroll, depth, lag, step):
    groups, lead = items // unroll, -(-(depth + lag) // unroll)
    assert lead < groups

    def group(g, fixed):
        for j in range(unroll):
            def at(s, j=j):
                slot = (j - s) % unroll
                if fixed:
                    i = g * unroll + j - s
                    return At(i, slot) if 0 <= i < items else None
                return At(g * unroll + (j - s), slot)
            step(j, at)

    for g in range(lead):
        group(g, True)
    with eng.Fori(lead, groups) as g:
        group(g, False)
    for g in range(groups, -(-(items + depth) // unroll)):
        group(g, True)


def stage_scope(nc):
    ctx = ExitStack()

    def sb(name, shape, dt=FP32):
        return ctx.enter_context(nc.sbuf_tensor(name, shape, dt))

    def sem(name):
        return ctx.enter_context(nc.semaphore(name))

    return ctx, sb, sem


def load_constants(nc, pairs):
    ctx, sb, sem = stage_scope(nc)
    with ctx:
        loaded = sem("constants_loaded")
        block = ctx.enter_context(nc.Block())

        @block.sync
        def _(sp):
            for dst, src in pairs:
                sp.dma_start(dst, src).then_inc(loaded, 16)
            sp.wait_ge(loaded, 16 * len(pairs))


def patch_embed(nc, images, x_main, x_tail, h, ps, w_tok, b_tok, pos, cls):
    n = CHUNK_IMAGES * PATCHES
    chunks = images // CHUNK_IMAGES
    pieces = 3
    kp = KT // pieces
    ctx, sb, sem = stage_scope(nc)
    with ctx:
        xb = sb("x_chunk", [P, 2, KT + 1, n])
        x_in = [[sem(f"x_in_{s}_{i}") for i in range(pieces)] for s in range(2)]
        tok_ps = sem("tok_ps")
        tok_done = sem("tok_done")
        cls_done = sem("cls_done")
        block = ctx.enter_context(nc.Block())

        @block.sync
        def _(sp):
            def step(j, at):
                a = at(0)
                if a:
                    if not (isinstance(a.index, int) and a.index < 2):
                        sp.wait_ge(tok_ps, a.index - 1)
                    for i in range(pieces):
                        sp.dma_start(xb[:, a.slot, i * kp:(i + 1) * kp, :],
                                     x_main[bass.ds(a.index, 1), :, i * kp:(i + 1) * kp, :]
                                     .rearrange("o p k n -> (o p) k n")).then_inc(x_in[a.slot][i], 16)
                    sp.dma_start(xb[0:KR, a.slot, KT, :],
                                 x_tail[bass.ds(a.index, 1), :, :]
                                 .rearrange("o p n -> (o p) n")).then_inc(x_in[a.slot][pieces - 1], 16)
            pipelined(sp, chunks, 2, 0, 2, step)

        @block.tensor
        def _(pe):
            def step(j, at):
                a = at(0)
                if a:
                    loads = (a.index - a.slot) // 2 + 1 if isinstance(a.index, int) else None
                    if not (isinstance(a.index, int) and a.index < 2):
                        pe.wait_ge(tok_done, a.index - 1)
                    for i in range(pieces):
                        per = 32 if i == pieces - 1 else 16
                        if loads is not None:
                            pe.wait_ge(x_in[a.slot][i], per * loads)
                        else:
                            pe.wait_ge(x_in[a.slot][i], (a.index - a.slot) * (per // 2) + per)
                        for k in range(i * kp, (i + 1) * kp):
                            nc.tensor.matmul(ps[:, a.slot, :], w_tok[:, k, :], xb[:, a.slot, k, :],
                                             start=(k == 0), stop=False)
                    nc.tensor.matmul(ps[:, a.slot, :], w_tok[0:KR, KT, :], xb[0:KR, a.slot, KT, :],
                                     start=False, stop=True).then_inc(tok_ps, 1)
            pipelined(pe, chunks, 2, 0, 2, step)

        @block.vector
        def _(dve):
            hv = h[:, :].rearrange("p (b t) -> p b t", t=SEQ)
            nc.vector.tensor_scalar(hv[:, :, 0], pos[:, 0:1].to_broadcast([P, images]), cls[:, 0:1],
                                    None, ALU.mult).then_inc(cls_done, 1)

            def step(j, at):
                a = at(0)
                if a:
                    dve.wait_ge(tok_ps, a.index + 1)
                    out = h[:, bass.ds(a.index * (CHUNK_IMAGES * SEQ), CHUNK_IMAGES * SEQ)]\
                        .rearrange("p (b t) -> p b t", t=SEQ)[:, :, 1:SEQ]
                    nc.vector.scalar_tensor_tensor(
                        out=out, in0=ps[:, a.slot, :].rearrange("p (b t) -> p b t", t=PATCHES),
                        scalar=b_tok[:, 0:1],
                        in1=pos[:, 1:SEQ].unsqueeze(1).to_broadcast([P, CHUNK_IMAGES, PATCHES]),
                        op0=ALU.add, op1=ALU.mult).then_inc(tok_done, 1)
            pipelined(dve, chunks, 2, 0, 2, step)


def layer_norm(nc, tag, tokens, h, xn, ps, mean_w):
    n = 416 if tokens % 832 == 0 else 260
    ctx, sb, sem = stage_scope(nc)
    with ctx:
        xc = sb(f"centered_{tag}", [P, 2, n])
        sq = sb(f"squared_{tag}", [P, 2, n])
        sd = sb(f"deviation_{tag}", [P, 2, n])
        rstd = sb(f"rstd_{tag}", [P, 2, n])
        eps = sb(f"eps_{tag}", [P, 1])
        eps_set = sem(f"eps_set_{tag}")
        mean_ps = sem(f"mean_ps_{tag}")
        centered = sem(f"centered_{tag}_s")
        squared = sem(f"squared_{tag}_s")
        var_ps = sem(f"var_ps_{tag}")
        sd_done = sem(f"sd_done_{tag}")
        rstd_done = sem(f"rstd_done_{tag}")
        normed = sem(f"normed_{tag}")
        block = ctx.enter_context(nc.Block())

        def cols(t, i):
            return t[:, bass.ds(i * n, n)]

        def started(i, lag):
            return not (isinstance(i, int) and i < lag)

        @block.tensor
        def _(pe):
            def step(j, at):
                a = at(0)
                if a:
                    if started(a.index, 2):
                        pe.wait_ge(centered, a.index - 1)
                    nc.tensor.matmul(ps[:, a.slot, 0:n], mean_w[:, :], cols(h, a.index),
                                     start=True, stop=True).then_inc(mean_ps, 1)
                a = at(1)
                if a:
                    pe.wait_ge(squared, a.index + 1)
                    nc.tensor.matmul(ps[:, 2 + a.slot, 0:n], mean_w[:, :], sq[:, a.slot, :],
                                     start=True, stop=True).then_inc(var_ps, 1)
            pipelined(pe, tokens // n, 2, 2, 2, step)

        @block.scalar
        def _(act):
            act.wait_ge(eps_set, 1)

            def step(j, at):
                a = at(2)
                if a:
                    act.wait_ge(var_ps, a.index + 1)
                    if started(a.index, 2):
                        act.wait_ge(rstd_done, a.index - 1)
                    nc.scalar.activation(sd[:, a.slot, :], ps[:, 2 + a.slot, 0:n], ACT.Sqrt,
                                         bias=eps[:, 0:1]).then_inc(sd_done, 1)
                a = at(0)
                if a:
                    act.wait_ge(centered, a.index + 1)
                    if started(a.index, 2):
                        act.wait_ge(var_ps, a.index - 1)
                        act.wait_ge(sd_done, a.index - 1)
                    nc.scalar.activation(sq[:, a.slot, :], xc[:, a.slot, :], ACT.Square)\
                        .then_inc(squared, 1)
            pipelined(act, tokens // n, 2, 2, 2, step)

        @block.vector
        def _(dve):
            nc.vector.memset(eps[:, :], EPS).then_inc(eps_set, 1)

            def step(j, at):
                a = at(2)
                if a:
                    dve.wait_ge(sd_done, a.index + 1)
                    if started(a.index, 2):
                        dve.wait_ge(normed, a.index - 1)
                    nc.vector.reciprocal(rstd[:, a.slot, :], sd[:, a.slot, :]).then_inc(rstd_done, 1)
                    dve.wait_ge(rstd_done, a.index + 1)
                    nc.vector.tensor_tensor(cols(xn, a.index), xc[:, a.slot, :], rstd[:, a.slot, :],
                                            ALU.mult).then_inc(normed, 1)
                a = at(0)
                if a:
                    dve.wait_ge(mean_ps, a.index + 1)
                    if started(a.index, 2):
                        dve.wait_ge(normed, a.index - 1)
                    nc.vector.tensor_tensor(xc[:, a.slot, :], cols(h, a.index), ps[:, a.slot, 0:n],
                                            ALU.subtract).then_inc(centered, 1)
            pipelined(dve, tokens // n, 2, 2, 2, step)


def attention(nc, tag, images, h, xn, ps, ident, w_qkv, w_out, b_out, order, b_qk=None, b_v=None,
              alphas_raw=None, w_dist=None, dist=None):
    masked = order > 1
    XS = 3 + order
    OS = XS + 2
    PAIR = 2 * SEQ
    ctx, sb, sem = stage_scope(nc)
    with ctx:
        xs = sb(f"xn_images_{tag}", [P, 4, SEQ])
        qk = sb(f"qk_{tag}", [P, 2, 2 * CH, PAIR])
        v = sb(f"v_{tag}", [SEQ, 4, H, DH + 1])
        shifted = sb(f"shifted_{tag}", [SEQ, 2, 2, CH, SEQ])
        e = sb(f"e_{tag}", [SEQ, 2, 2, CH, SEQ])
        neg_max = sb(f"neg_max_{tag}", [SEQ, 2, 2, CH])
        et = sb(f"eT_{tag}", [SEQ, 4, 2, CH, SEQ])
        inv = sb(f"inv_sum_{tag}", [SEQ, 4, H])
        res = sb(f"res_{tag}", [SEQ, 2, INNER])
        res_t = sb(f"resT_{tag}", [P, 2, CH, PAIR])
        if masked:
            neg_s = sb(f"neg_scores_{tag}", [SEQ, 2, 2, CH, SEQ])
            low8 = sb(f"low8_{tag}", [SEQ, 2, 2, CH, 8])
            least = sb(f"least_kept_{tag}", [SEQ, 2, 2, CH])
            keep = sb(f"keep_{tag}", [SEQ, 2, 2, CH, SEQ])
            em = sb(f"e_masked_{tag}", [SEQ, 2, 2, CH, SEQ])
            al = sb(f"alphas_{tag}", [SEQ, ORDER, H])
            inv_a = sb(f"inv_sum_alpha_{tag}", [SEQ, 2, H])
            va = sb(f"v_alpha_{tag}", [SEQ, 2, 4, H, DH])
            tv = sb(f"Av_{tag}", [SEQ, 2, 2, H, DH])
            cv = sb(f"horner_{tag}", [SEQ, 2, 2, H, DH])
        else:
            em = e
            wv = sb(f"dist_values_{tag}", [SEQ, 4, D])

        def s(name):
            return sem(f"{name}_{tag}")
        ones_set, alphas_set = s("ones_set"), s("alphas_set")
        xs_copied = s("xs_copied")
        qk_ps, qk_sb = s("qk_ps"), s("qk_sb")
        v_ps, v_sb, va_done = s("v_ps"), s("v_sb"), s("va_done")
        s_ps, neg_done, low_done = s("s_ps"), s("neg_done"), s("low_done")
        max_done, least_done, keep_done = s("max_done"), s("least_done"), s("keep_done")
        shift_done, exp_done = s("shift_done"), s("exp_done")
        em_done = s("em_done") if masked else exp_done
        t_ps, et_sb = s("t_ps"), s("et_sb")
        inv_done, inv_a_done = s("inv_done"), s("inv_a_done")
        r_ps = [s(f"r{n}_ps") for n in range(order)]
        r_sb = [s(f"r{n}_sb") for n in range(order)]
        c_done = [s(f"c{n}_done") for n in range(2)]
        x_ps, x_sb = s("x_ps"), s("x_sb")
        w_ps, w_sb = s("w_ps"), s("w_sb")
        o_ps, o_added = s("o_ps"), s("o_added")
        block = ctx.enter_context(nc.Block())

        def since(eng, sm, index, lag, more=0):
            if not (isinstance(index, int) and index < lag):
                eng.wait_ge(sm, index - lag + 1 + more)

        def scores(i=None):
            return ps[0:SEQ, 0:2, 0:CH * SEQ].rearrange("p b (c k) -> p b c k", k=SEQ)

        def natural(t):
            return t.rearrange("p (c b) d -> p b c d", b=2)

        def over_d(t):
            return t.unsqueeze(2).to_broadcast([SEQ, H, DH])

        @block.gpsimd
        def _(pool):
            nc.gpsimd.memset(v[:, :, :, DH:DH + 1], 1.0).then_inc(ones_set, 1)
            if masked:
                pool.wait_ge(alphas_set, 1)

            def step(j, at):
                a = at(0)
                if a and j % 2 == 0:
                    since(pool, v_ps, a.index, 4, 1)
                    if not masked:
                        since(pool, w_ps, a.index, 4, 1)
                    nc.gpsimd.tensor_copy(xs[:, a.slot:a.slot + 2, :].rearrange("p a t -> p (a t)"),
                                          xn[:, bass.ds(a.index * SEQ, PAIR)]).then_inc(xs_copied, 2)
                if not masked:
                    return
                a = at(3)
                if a:
                    pool.wait_ge(r_sb[0], a.index + 1)
                    since(pool, r_ps[1], a.index, 2)
                    nc.gpsimd.tensor_tensor(cv[:, 0, a.slot % 2], tv[:, 0, a.slot % 2],
                                            va[:, 1, a.slot], ALU.add).then_inc(c_done[0], 1)
                a = at(1)
                if a:
                    pool.wait_ge(exp_done, a.index + 1)
                    pool.wait_ge(keep_done, a.index + 1)
                    since(pool, t_ps, a.index, 2)
                    nc.gpsimd.tensor_tensor(em[:, a.slot % 2], e[:, a.slot % 2], keep[:, a.slot % 2],
                                            ALU.mult).then_inc(em_done, 1)
                a = at(4)
                if a:
                    pool.wait_ge(r_sb[1], a.index + 1)
                    since(pool, r_ps[2], a.index, 2)
                    nc.gpsimd.tensor_tensor(cv[:, 1, a.slot % 2], tv[:, 1, a.slot % 2],
                                            va[:, 0, a.slot], ALU.add).then_inc(c_done[1], 1)
                a = at(2)
                if a:
                    pool.wait_ge(v_sb, a.index + 1)
                    since(pool, c_done[1], a.index, 4)
                    for n in range(2):
                        nc.gpsimd.tensor_tensor(va[:, n, a.slot], v[:, a.slot, :, 0:DH],
                                                over_d(al[:, n, :]), ALU.mult).then_inc(va_done, 1)
                    pool.wait_ge(va_done, 2 * a.index + 2)
            pipelined(pool, images, 4, OS, 4, step)

        @block.scalar
        def _(act):
            if masked:
                nc.scalar.activation(al[:, :, :], alphas_raw, ACT.Gelu).then_inc(alphas_set, 1)

            def qk_out(a, m):
                act.wait_ge(qk_ps, 2 * a.index + m + 1)
                if m == 0:
                    since(act, s_ps, a.index, 4, 1)
                for n, c in enumerate((m, CH + m)):
                    last = nc.scalar.activation(
                        qk[:, a.slot // 2, c, :], ps[:, 4 + m % 2, n * PAIR:(n + 1) * PAIR],
                        ACT.Identity, bias=b_qk[:, c:c + 1] if b_qk is not None else 0.0)
                last.then_inc(qk_sb, 1)

            def step(j, at):
                a = at(0)
                if a and j % 2 == 0:
                    qk_out(a, 0)
                    qk_out(a, 1)
                a = at(1)
                if a and masked:
                    act.wait_ge(s_ps, a.index + 1)
                    nc.scalar.activation(neg_s[:, a.slot % 2], scores(), ACT.Copy, scale=-1.0)\
                        .then_inc(neg_done, 1)
                a = at(0)
                if a and j % 2 == 0:
                    qk_out(a, 2)
                    qk_out(a, 3)
                a = at(2)
                if a:
                    act.wait_ge(t_ps, a.index + 1)
                    since(act, r_ps[-1], a.index, 4)
                    nc.scalar.activation(
                        et[:, a.slot], ps[0:SEQ, 2:4, 0:CH * SEQ].rearrange("p b (c k) -> p b c k", k=SEQ),
                        ACT.Copy).then_inc(et_sb, 1)
                    if not masked:
                        act.wait_ge(w_ps, a.index + 1)
                        since(act, o_ps, a.index - a.slot % 2, 4, 1)
                        nc.scalar.activation(wv[:, a.slot], ps[0:SEQ, 3, BANK - D:BANK], ACT.Copy)\
                            .then_inc(w_sb, 1)
                a = at(1)
                if a:
                    act.wait_ge(shift_done, a.index + 1)
                    since(act, em_done if masked else t_ps, a.index, 2)
                    nc.scalar.activation(e[:, a.slot % 2], shifted[:, a.slot % 2], ACT.Exp, scale=SCALE)\
                        .then_inc(exp_done, 1)
                a = at(XS)
                if a:
                    act.wait_ge(x_ps, a.index + 1)
                    since(act, o_ps, a.index - a.slot % 2, 4, 1)
                    nc.scalar.activation(
                        res_t[:, a.slot // 2, :, (a.slot % 2) * SEQ:(a.slot % 2 + 1) * SEQ],
                        ps[:, 5, 0:CH * SEQ].rearrange("p (c q) -> p c q", q=SEQ), ACT.Copy)\
                        .then_inc(x_sb, 1)
            pipelined(act, images, 4, OS, 4, step)

        @block.vector
        def _(dve):
            dve.wait_ge(ones_set, 1)
            if masked:
                dve.wait_ge(alphas_set, 1)

            def read_out(n, a, factor):
                dve.wait_ge(r_ps[n], a.index + 1)
                if n < order - 1:
                    since(dve, c_done[n], a.index, 2)
                    dst = tv[:, n, a.slot % 2]
                else:
                    since(dve, x_ps, a.index, 2)
                    dst = res[:, a.slot % 2].rearrange("p (h d) -> p h d", d=DH)
                if n == 0:
                    src = ps[0:SEQ, 6:8, 0:CH * (DH + 1)]\
                        .rearrange("p b (c d) -> p b c d", d=DH + 1)[:, :, :, 0:DH]
                    last = nc.vector.tensor_tensor(natural(dst), src, natural(over_d(factor)), ALU.mult)
                else:
                    src = ps[0:SEQ, 5 + n, :].rearrange("p (h d) -> p h d", d=DH)
                    last = nc.vector.tensor_tensor(dst, src, over_d(factor), ALU.mult)
                last.then_inc(r_sb[n], 1)

            def step(j, at):
                a = at(OS)
                if a and j % 2 == 0:
                    dve.wait_ge(o_ps, a.index + 2)
                    hp = h[:, bass.ds(a.index * SEQ, PAIR)]
                    nc.vector.scalar_tensor_tensor(out=hp, in0=ps[:, 4, 0:PAIR], scalar=b_out[:, 0:1],
                                                   in1=hp, op0=ALU.add, op1=ALU.add).then_inc(o_added, 2)
                a = at(3)
                if a:
                    dve.wait_ge(r_ps[0], a.index + 1)
                    nc.vector.reciprocal(
                        inv[:, a.slot, :].rearrange("p (c b) -> p b c", b=2),
                        ps[0:SEQ, 6:8, 0:CH * (DH + 1)]
                        .rearrange("p b (c d) -> p b c d", d=DH + 1)[:, :, :, DH]).then_inc(inv_done, 1)
                    dve.wait_ge(inv_done, a.index + 1)
                    if masked:
                        nc.vector.tensor_tensor(inv_a[:, a.slot % 2, :], inv[:, a.slot, :],
                                                al[:, ORDER - 1, :], ALU.mult).then_inc(inv_a_done, 1)
                        dve.wait_ge(inv_a_done, a.index + 1)
                        read_out(0, a, inv_a[:, a.slot % 2, :])
                    else:
                        read_out(0, a, inv[:, a.slot, :])
                a = at(1)
                if a:
                    dve.wait_ge(s_ps, a.index + 1)
                    if masked:
                        dve.wait_ge(neg_done, a.index + 1)
                    nc.vector.tensor_reduce(neg_max[:, a.slot % 2], scores(), AX.X, ALU.max,
                                            negate=True).then_inc(max_done, 1)
                    dve.wait_ge(max_done, a.index + 1)
                    since(dve, exp_done, a.index, 2)
                    nc.vector.tensor_tensor(
                        shifted[:, a.slot % 2], scores(),
                        neg_max[:, a.slot % 2].unsqueeze(3).to_broadcast([SEQ, 2, CH, SEQ]),
                        ALU.add).then_inc(shift_done, 1)
                    if masked:
                        for b in range(2):
                            for c in range(CH):
                                last = nc.vector.max(low8[:, a.slot % 2, b, c, :],
                                                     neg_s[:, a.slot % 2, b, c, :])
                        last.then_inc(low_done, 1)
                        dve.wait_ge(low_done, a.index + 1)
                        nc.vector.tensor_scalar(least[:, a.slot % 2], low8[:, a.slot % 2, :, :, 1],
                                                -1.0, None, ALU.mult).then_inc(least_done, 1)
                        dve.wait_ge(least_done, a.index + 1)
                        since(dve, em_done, a.index, 2)
                        nc.vector.tensor_tensor(
                            keep[:, a.slot % 2], scores(),
                            least[:, a.slot % 2].unsqueeze(3).to_broadcast([SEQ, 2, CH, SEQ]),
                            ALU.is_ge).then_inc(keep_done, 1)
                a = at(4)
                if a and masked:
                    read_out(1, a, inv[:, a.slot, :])
                a = at(2)
                if a:
                    dve.wait_ge(v_ps, a.index + 1)
                    since(dve, r_ps[0], a.index, 4)
                    if masked:
                        since(dve, va_done, a.index, 4, a.index - 3)
                    dst = v[:, a.slot, :, 0:DH]
                    src = ps[0:SEQ, 4, :].rearrange("p (h d) -> p h d", d=DH)
                    if b_v is not None:
                        last = nc.vector.tensor_tensor(
                            dst, src, b_v.rearrange("p (h d) -> p h d", d=DH), ALU.add)
                    else:
                        last = nc.vector.tensor_copy(dst, src)
                    last.then_inc(v_sb, 1)
                a = at(5)
                if a and masked:
                    read_out(2, a, inv[:, a.slot, :])
            pipelined(dve, images, 4, OS, 4, step)

        @block.tensor
        def _(pe):
            def project_qk(a, m, at):
                pe.wait_ge(xs_copied, a.index + 2)
                if m < 2:
                    if m == 0:
                        if at(OS):
                            pe.wait_ge(o_added, at(OS).index + 2)
                        elif at(3):
                            pe.wait_ge(v_sb, at(3).index + 1)
                    elif at(XS + 1):
                        pe.wait_ge(x_sb, at(XS + 1).index + 1)
                else:
                    pe.wait_ge(qk_sb, 2 * a.index + m - 1)
                for n, c in enumerate((m, CH + m)):
                    last = nc.tensor.matmul(ps[:, 4 + m % 2, n * PAIR:(n + 1) * PAIR],
                                            w_qkv[:, c * P:(c + 1) * P],
                                            xs[:, a.slot:a.slot + 2, :].rearrange("p a t -> p (a t)"),
                                            start=True, stop=True)
                last.then_inc(qk_ps, 1)

            def product(n, a):
                for hd in range(H):
                    c, b = hd // 2, hd % 2
                    if n == 0:
                        out = ps[0:SEQ, 6 + b, c * (DH + 1):(c + 1) * (DH + 1)]
                        rhs = v[:, a.slot, hd, :]
                    else:
                        out = ps[0:SEQ, 5 + n, hd * DH:(hd + 1) * DH]
                        rhs = cv[:, n - 1, a.slot % 2, hd, :]
                    last = nc.tensor.matmul(out, et[:, a.slot, b, c, :], rhs, start=True, stop=True)
                last.then_inc(r_ps[n], 1)

            def step(j, at):
                even = j % 2 == 0
                a = at(OS)
                if a and even:
                    pe.wait_ge(x_sb, a.index + 2)
                    if at(3):
                        pe.wait_ge(v_sb, at(3).index + 1)
                    elif not (isinstance(a.index, int) and a.index < 2):
                        pe.wait_ge(o_added, a.index)
                    for c in range(CH):
                        last = nc.tensor.matmul(ps[:, 4, 0:PAIR], w_out[:, c, :], res_t[:, a.slot // 2, c, :],
                                                start=(c == 0), stop=(masked and c == CH - 1))
                    if not masked:
                        pe.wait_ge(w_sb, a.index + 2)
                        for n in range(2):
                            last = nc.tensor.matmul(ps[:, 4, n * SEQ:(n + 1) * SEQ], wv[:, a.slot + n, :],
                                                    dist[0:SEQ, :], start=False, stop=(n == 1))
                    last.then_inc(o_ps, 2)
                a = at(3)
                if a:
                    pe.wait_ge(et_sb, a.index + 1)
                    pe.wait_ge(v_sb, a.index + 1)
                    if masked:
                        since(pe, r_sb[1], a.index, 2)
                        since(pe, r_sb[2], a.index, 3)
                    else:
                        since(pe, r_sb[0], a.index, 1)
                    product(0, a)
                a = at(0)
                if a and even:
                    project_qk(a, 0, at)
                    project_qk(a, 1, at)
                a = at(1)
                if a:
                    pe.wait_ge(qk_sb, 2 * (a.index - a.slot % 2) + 4)
                    since(pe, shift_done, a.index, 1)
                    if masked:
                        since(pe, keep_done, a.index, 1)
                        since(pe, neg_done, a.index, 1)
                    for hd in range(H):
                        c, b = hd // 2, hd % 2
                        rows = slice(b * DH, (b + 1) * DH)
                        cols = slice((a.slot % 2) * SEQ, (a.slot % 2 + 1) * SEQ)
                        last = nc.tensor.matmul(ps[0:SEQ, b, c * SEQ:(c + 1) * SEQ],
                                                qk[rows, a.slot // 2, c, cols],
                                                qk[rows, a.slot // 2, CH + c, cols],
                                                start=True, stop=True)
                    last.then_inc(s_ps, 1)
                a = at(0)
                if a and even:
                    project_qk(a, 2, at)
                    project_qk(a, 3, at)
                a = at(4)
                if a and masked:
                    pe.wait_ge(c_done[0], a.index + 1)
                    if at(3):
                        pe.wait_ge(r_sb[0], at(3).index + 1)
                    else:
                        since(pe, r_sb[1], a.index, 1)
                    product(1, a)
                a = at(2)
                if a:
                    pe.wait_ge(xs_copied, a.index - a.slot % 2 + 2)
                    if even:
                        if at(0):
                            pe.wait_ge(qk_sb, 2 * at(0).index + 3)
                        elif at(OS):
                            pe.wait_ge(o_added, at(OS).index + 2)
                    else:
                        since(pe, v_sb, a.index, 1)
                    nc.tensor.matmul(ps[0:SEQ, 4, :], xs[:, a.slot, :], w_qkv[:, 2 * INNER:3 * INNER],
                                     start=True, stop=True).then_inc(v_ps, 1)
                    if not masked:
                        since(pe, w_sb, a.index, 1)
                        since(pe, et_sb, a.index, 1)
                        nc.tensor.matmul(ps[0:SEQ, 3, BANK - D:BANK], xs[:, a.slot, :], w_dist[:, :],
                                         start=True, stop=True).then_inc(w_ps, 1)
                a = at(2)
                if a:
                    pe.wait_ge(em_done, a.index + 1)
                    since(pe, et_sb, a.index, 1)
                    for b in range(2):
                        for c in range(CH):
                            last = nc.tensor.transpose(ps[0:SEQ, 2 + b, c * SEQ:(c + 1) * SEQ],
                                                       em[:, a.slot % 2, b, c, :], ident[0:SEQ, 0:SEQ])
                    last.then_inc(t_ps, 1)
                a = at(5)
                if a and masked:
                    pe.wait_ge(c_done[1], a.index + 1)
                    if not at(3):
                        since(pe, r_sb[2], a.index, 1)
                    product(2, a)
                a = at(XS)
                if a:
                    pe.wait_ge(r_sb[-1], a.index + 1)
                    if even and at(0):
                        pe.wait_ge(qk_sb, 2 * at(0).index + 4)
                    else:
                        since(pe, x_sb, a.index, 1)
                    for c in range(CH):
                        last = nc.tensor.transpose(ps[:, 5, c * SEQ:(c + 1) * SEQ],
                                                   res[:, a.slot % 2, c * P:(c + 1) * P],
                                                   ident[0:SEQ, 0:SEQ])
                    last.then_inc(x_ps, 1)
            pipelined(pe, images, 4, OS, 4, step)


def route_with_capacity(nc, tokens, xn, ps, router, expert_ids, before, all_ones, ident, gate_all):
    n = P if tokens % P == 0 else 104
    SL = 2
    ctx, sb, sem = stage_scope(nc)
    with ctx:
        xs = sb("xn_tile_r", [P, SL, n])
        held = sb("held_r", [P, 1])
        top = sb("top8_r", [P, SL, 8])
        idx = sb("index8_r", [P, SL, 8], U32)
        idf = sb("index_r", [P, SL, 2])
        nm = sb("neg_max_r", [P, SL, 1])
        prob = sb("prob_r", [P, SL, E0])
        psum_ = sb("prob_sum_r", [P, SL, 1])
        inv = sb("inv_sum_r", [P, SL, 1])
        first = sb("first_choice", [P, SL, E0])
        both = sb("both_choices", [P, SL, E0], BF16)
        count = sb("count_before", [P, SL, E0])
        carry = sb("count_carry", [P, E0])
        kept = sb("kept_choice", [P, SL, E0])
        scratch = sb("gate_terms", [P, SL, E0])
        gate = sb("gate_r", [P, SL, 1])
        gate_w = sb("gate_wide", [P, SL, P])
        copied, l_ps = sem("xs_copied_r"), sem("logits_ps_r")
        top_done, idx_done, idf_done = sem("top_done_r"), sem("idx_done_r"), sem("idf_done_r")
        nm_done, prob_done = sem("nm_done_r"), sem("prob_done_r")
        first_done, both_done = sem("first_done_r"), sem("both_done_r")
        rank_ps, carry_set, carry_done = sem("rank_ps_r"), sem("carry_set_r"), sem("carry_done_r")
        count_done, kept_done, terms_done = sem("count_done_r"), sem("kept_done_r"), sem("terms_r")
        gate_done, inv_done, wide_done = sem("gate_done_r"), sem("inv_done_r"), sem("wide_done_r")
        bc_ps, bc_done = sem("gate_ps_r"), sem("gate_all_done_r")
        block = ctx.enter_context(nc.Block())
        D_ = 2

        def since(eng, sm, index, lag):
            if not (isinstance(index, int) and index < lag):
                eng.wait_ge(sm, index - lag + 1)

        def logits(slot):
            return ps[0:n, slot, 0:E0]

        def ranks(slot, part):
            return ps[0:n, 2 + slot, part * E0:(part + 1) * E0]

        @block.gpsimd
        def _(pool):
            def step(j, at):
                a = at(0)
                if a:
                    since(pool, l_ps, a.index, SL)
                    nc.gpsimd.tensor_copy(xs[:, a.slot, :], xn[:, bass.ds(a.index * n, n)])\
                        .then_inc(copied, 1)
            pipelined(pool, tokens // n, SL, D_, SL, step)

        @block.tensor
        def _(pe):
            def step(j, at):
                a = at(0)
                if a:
                    pe.wait_ge(copied, a.index + 1)
                    since(pe, prob_done, a.index, SL)
                    since(pe, idx_done, a.index, SL)
                    nc.tensor.matmul(logits(a.slot), xs[:, a.slot, :], router[:, :],
                                     start=True, stop=True).then_inc(l_ps, 1)
                a = at(1)
                if a:
                    pe.wait_ge(both_done, a.index + 1)
                    since(pe, carry_done, a.index, SL)
                    nc.tensor.matmul(ranks(a.slot, 0), before[0:n, 0:n], both[0:n, a.slot, :],
                                     start=True, stop=True)
                    nc.tensor.matmul(ranks(a.slot, 1), all_ones[0:n, 0:n], both[0:n, a.slot, :],
                                     start=True, stop=True).then_inc(rank_ps, 1)
                a = at(2)
                if a:
                    pe.wait_ge(wide_done, a.index + 1)
                    since(pe, bc_done, a.index, SL)
                    nc.tensor.matmul(ps[:, 4 + a.slot, 0:n], gate_w[0:n, a.slot, :], ident[0:n, 0:n],
                                     start=True, stop=True).then_inc(bc_ps, 1)
            pipelined(pe, tokens // n, SL, D_, SL, step)

        @block.scalar
        def _(act):
            def step(j, at):
                a = at(0)
                if a:
                    act.wait_ge(nm_done, a.index + 1)
                    act.wait_ge(idx_done, a.index + 1)
                    since(act, terms_done, a.index, SL)
                    since(act, inv_done, a.index, SL)
                    nc.scalar.activation(prob[0:n, a.slot, :], logits(a.slot), ACT.Exp,
                                         bias=nm[0:n, a.slot, :], accum_out=psum_[0:n, a.slot, :])\
                        .then_inc(prob_done, 1)
                a = at(2)
                if a:
                    act.wait_ge(bc_ps, a.index + 1)
                    nc.scalar.activation(gate_all[:, bass.ds(a.index * n, n)], ps[:, 4 + a.slot, 0:n],
                                         ACT.Copy).then_inc(bc_done, 1)
            pipelined(act, tokens // n, SL, D_, SL, step)

        @block.vector
        def _(dve):
            nc.vector.memset(carry[:, :], 0.0).then_inc(carry_set, 1)

            def step(j, at):
                a = at(0)
                if a:
                    i, sl = a.index, a.slot
                    dve.wait_ge(l_ps, i + 1)
                    nc.vector.memset(held[:, :], 0.0)
                    nc.vector.max(top[0:n, sl, :], logits(sl)).then_inc(top_done, 1)
                    dve.wait_ge(top_done, i + 1)
                    since(dve, prob_done, i, SL)
                    nc.vector.tensor_scalar(nm[0:n, sl, :], top[0:n, sl, 0:1], -1.0, None, ALU.mult)\
                        .then_inc(nm_done, 1)
                    nc.vector.max_index(idx[0:n, sl, :], top[0:n, sl, :], logits(sl))\
                        .then_inc(idx_done, 1)
                    dve.wait_ge(idx_done, i + 1)
                    nc.vector.tensor_copy(idf[0:n, sl, :], idx[0:n, sl, 0:2]).then_inc(idf_done, 1)
                    dve.wait_ge(idf_done, i + 1)
                    nc.vector.tensor_scalar(first[0:n, sl, :], expert_ids[0:n, :], idf[0:n, sl, 0:1],
                                            None, ALU.is_equal).then_inc(first_done, 1)
                    dve.wait_ge(first_done, i + 1)
                    since(dve, rank_ps, i, SL)
                    nc.vector.scalar_tensor_tensor(out=both[0:n, sl, :], in0=expert_ids[0:n, :],
                                                   scalar=idf[0:n, sl, 1:2], in1=first[0:n, sl, :],
                                                   op0=ALU.is_equal, op1=ALU.add).then_inc(both_done, 1)
                a = at(1)
                if a:
                    i, sl = a.index, a.slot
                    dve.wait_ge(rank_ps, i + 1)
                    dve.wait_ge(carry_set, 1)
                    since(dve, carry_done, i, 1)
                    nc.vector.tensor_tensor(count[0:n, sl, :], ranks(sl, 0), carry[0:n, :], ALU.add)\
                        .then_inc(count_done, 1)
                    dve.wait_ge(count_done, i + 1)
                    nc.vector.tensor_tensor(carry[0:n, :], ranks(sl, 1), carry[0:n, :], ALU.add)\
                        .then_inc(carry_done, 1)
                    nc.vector.scalar_tensor_tensor(out=kept[0:n, sl, :], in0=count[0:n, sl, :],
                                                   scalar=float(CAPACITY), in1=both[0:n, sl, :],
                                                   op0=ALU.is_lt, op1=ALU.mult).then_inc(kept_done, 1)
                    dve.wait_ge(kept_done, i + 1)
                    dve.wait_ge(prob_done, i + 1)
                    nc.vector.tensor_tensor_reduce(out=scratch[0:n, sl, :], in0=kept[0:n, sl, :],
                                                   in1=prob[0:n, sl, :], scale=1.0, scalar=0.0,
                                                   op0=ALU.mult, op1=ALU.add,
                                                   accum_out=gate[0:n, sl, :]).then_inc(terms_done, 1)
                    nc.vector.reciprocal(inv[0:n, sl, :], psum_[0:n, sl, :]).then_inc(inv_done, 1)
                    dve.wait_ge(inv_done, i + 1)
                    dve.wait_ge(terms_done, i + 1)
                    since(dve, bc_ps, i, SL)
                    nc.vector.tensor_scalar(gate_w[0:n, sl, :],
                                            gate[0:n, sl, :].to_broadcast([n, P]),
                                            inv[0:n, sl, :], None, ALU.mult).then_inc(wide_done, 1)
            pipelined(dve, tokens // n, SL, D_, SL, step)


def shared_mlp(nc, tokens, h, xn, ps, w1, b1, w2, b2, gate_all):
    n = 416 if tokens % 832 == 0 else 260
    C = F0 // P
    ctx, sb, sem = stage_scope(nc)
    with ctx:
        g1 = sb("gelu_out", [P, 2, C, n])
        y = sb("mlp_gated", [P, 2, n])
        up_ps, g_done = sem("up_ps"), sem("gelu_done")
        y_ps, y_done, h_done = sem("down_ps"), sem("gated"), sem("h_added")
        block = ctx.enter_context(nc.Block())

        def since(eng, sm, index, lag):
            if not (isinstance(index, int) and index < lag):
                eng.wait_ge(sm, index - lag + 1)

        @block.tensor
        def _(pe):
            def step(j, at):
                a = at(0)
                if a:
                    for c in range(C):
                        if not (isinstance(a.index, int) and a.index < 1):
                            pe.wait_ge(g_done, C * a.index - C + c + 1)
                        nc.tensor.matmul(ps[:, c, 0:n], w1[:, c * P:(c + 1) * P],
                                         xn[:, bass.ds(a.index * n, n)], start=True, stop=True)\
                            .then_inc(up_ps, 1)
                a = at(1)
                if a:
                    pe.wait_ge(g_done, C * a.index + C)
                    since(pe, y_done, a.index, 2)
                    for c in range(C):
                        last = nc.tensor.matmul(ps[:, 4 + a.slot, 0:n], w2[:, c, :], g1[:, a.slot, c, :],
                                                start=(c == 0), stop=(c == C - 1))
                    last.then_inc(y_ps, 1)
            pipelined(pe, tokens // n, 2, 1, 2, step)

        @block.scalar
        def _(act):
            def step(j, at):
                a = at(0)
                if a:
                    since(act, y_ps, a.index, 2)
                    for c in range(C):
                        act.wait_ge(up_ps, C * a.index + c + 1)
                        nc.scalar.activation(g1[:, a.slot, c, :], ps[:, c, 0:n], ACT.Gelu,
                                             bias=b1[:, c:c + 1]).then_inc(g_done, 1)
            pipelined(act, tokens // n, 2, 1, 2, step)

        @block.vector
        def _(dve):
            def step(j, at):
                a = at(1)
                if a:
                    cols = bass.ds(a.index * n, n)
                    dve.wait_ge(y_ps, a.index + 1)
                    nc.vector.scalar_tensor_tensor(out=y[:, a.slot, :], in0=ps[:, 4 + a.slot, 0:n],
                                                   scalar=b2[:, 0:1], in1=gate_all[:, cols],
                                                   op0=ALU.add, op1=ALU.mult).then_inc(y_done, 1)
                    dve.wait_ge(y_done, a.index + 1)
                    nc.vector.tensor_tensor(h[:, cols], h[:, cols], y[:, a.slot, :], ALU.add)\
                        .then_inc(h_done, 1)
            pipelined(dve, tokens // n, 2, 1, 2, step)


def dense_mixture(nc, tokens, h, xn, ps, ident, gate_w, gate_b, expert_ids, w1, b1, w2, b2, out):
    n = P if tokens % P == 0 else 104
    SL = 2
    C = F1 // P * E1
    HB = 4
    ctx, sb, sem = stage_scope(nc)
    with ctx:
        xs = sb("xn_tile_m", [P, SL, n])
        held = sb("held_m", [P, 1])
        hs = sb("h_tile_m", [P, SL, n])
        logit = sb("logit_m", [P, SL, E1])
        top = sb("top8_m", [P, SL, 8])
        idx = sb("index8_m", [P, SL, 8], U32)
        idf = sb("index_m", [P, SL, 2])
        gap = sb("gap_m", [P, SL, 1])
        eg = sb("exp_gap_m", [P, SL, 1])
        ws = sb("weight_sum_m", [P, SL, 1])
        wa = sb("weight_first_m", [P, SL, 1])
        wb = sb("weight_second_m", [P, SL, 1])
        first = sb("first_weight_m", [P, SL, E1])
        wt = sb("weights_m", [P, SL, E1])
        wtt = sb("weightsT_m", [E1, SL, n])
        hid = sb("hidden_m", [P, SL, C, n])
        acc = sb("acc_m", [P, SL, D])
        copied, l_ps = sem("copied_m"), sem("logits_ps_m")
        dstep = sem("weight_steps_m")
        gap_done, eg_done, wt_done = sem("gap_done_m"), sem("eg_done_m"), sem("wt_done_m")
        wtt_ps, wtt_sb = sem("wT_ps_m"), sem("wT_sb_m")
        base_ps, base_sb = sem("base_ps_m"), sem("base_sb_m")
        hid_ps, hid_sb = sem("hid_ps_m"), sem("hid_sb_m")
        y_ps, acc_done = sem("y_ps_m"), sem("acc_done_m")
        stored = [sem(f"stored_m{i}") for i in range(SL)]
        block = ctx.enter_context(nc.Block())
        NB = C // HB
        D_ = 2
        STEPS = 8

        def since(eng, sm, index, lag, per=1):
            if not (isinstance(index, int) and index < lag):
                eng.wait_ge(sm, index * per - (lag - 1) * per)

        def base_bank(slot):
            return ps[0:n, 4 + slot, 0:D]

        def wtt_bank(slot):
            return ps[0:E1, 7, 0:n]

        @block.sync
        def _(sp):
            def step(j, at):
                a = at(2)
                if a:
                    sp.wait_ge(acc_done, E1 * a.index + E1)
                    sp.dma_start(out[bass.ds(a.index * n, n), :], acc[0:n, a.slot, :])\
                        .then_inc(stored[a.slot], 16)
            pipelined(sp, tokens // n, SL, D_, SL, step)
            for i in range(SL):
                sp.wait_ge(stored[i], 16 * len(range(i, tokens // n, SL)))

        @block.gpsimd
        def _(pool):
            def step(j, at):
                a = at(0)
                if a:
                    since(pool, l_ps, a.index, SL)
                    since(pool, base_ps, a.index, SL)
                    cols = bass.ds(a.index * n, n)
                    nc.gpsimd.tensor_copy(xs[:, a.slot, :], xn[:, cols])
                    nc.gpsimd.tensor_copy(hs[:, a.slot, :], h[:, cols]).then_inc(copied, 1)
            pipelined(pool, tokens // n, SL, D_, SL, step)

        @block.tensor
        def _(pe):
            def up(a, b):
                if b >= 2:
                    pe.wait_ge(hid_sb, NB * a.index + b - 1)
                elif not (isinstance(a.index, int) and a.index < 1):
                    pe.wait_ge(hid_sb, NB * a.index + b - 1)
                for i in range(HB):
                    c = b * HB + i
                    last = nc.tensor.matmul(ps[:, b % 2, i * P:i * P + n], w1[:, c * P:(c + 1) * P],
                                            xn[:, bass.ds(a.index * n, n)], start=True, stop=True)
                last.then_inc(hid_ps, 1)

            def down(a, b):
                pe.wait_ge(hid_sb, NB * a.index + (b + 1) * (NB // 2))
                if not (isinstance(a.index, int) and a.index < 1):
                    pe.wait_ge(acc_done, E1 * a.index - E1 + (b + 1) * (E1 // 2))
                for e in range(b * E1 // 2, (b + 1) * E1 // 2):
                    for f in range(F1 // P):
                        c = e * (F1 // P) + f
                        last = nc.tensor.matmul(ps[0:n, 2 + b, (e % 4) * D:(e % 4 + 1) * D],
                                                hid[:, a.slot, c, :], w2[:, c, :],
                                                start=(f == 0), stop=(f == F1 // P - 1))
                last.then_inc(y_ps, 1)

            def step(j, at):
                a = at(0)
                if a:
                    pe.wait_ge(copied, a.index + 1)
                    since(pe, dstep, a.index, 1, STEPS)
                    nc.tensor.matmul(ps[0:n, 6, 0:E1], xs[:, a.slot, :],
                                     gate_w[:, :], start=True, stop=True).then_inc(l_ps, 1)
                    up(a, 0)
                    up(a, 1)
                b = at(1)
                if b:
                    pe.wait_ge(wt_done, b.index + 1)
                    since(pe, wtt_sb, b.index, 1)
                    nc.tensor.transpose(wtt_bank(b.slot), wt[0:n, b.slot, :], ident[0:n, 0:n])\
                        .then_inc(wtt_ps, 1)
                if b:
                    down(b, 0)
                if a:
                    up(a, 2)
                if b:
                    pe.wait_ge(wtt_sb, b.index + 1)
                    since(pe, base_sb, b.index, SL)
                    nc.tensor.matmul(base_bank(b.slot), hs[:, b.slot, :], ident[:, :],
                                     start=True, stop=False)
                    nc.tensor.matmul(base_bank(b.slot), wtt[:, b.slot, :], b2[0:E1, :],
                                     start=False, stop=True).then_inc(base_ps, 1)
                    down(b, 1)
                if a:
                    up(a, 3)
            pipelined(pe, tokens // n, SL, D_, SL, step)

        @block.scalar
        def _(act):
            def relu(a, b):
                act.wait_ge(hid_ps, NB * a.index + b + 1)
                if b == 0:
                    since(act, y_ps, a.index, SL, 2)
                for i in range(HB):
                    c = b * HB + i
                    last = nc.scalar.activation(hid[:, a.slot, c, :], ps[:, b % 2, i * P:i * P + n],
                                                ACT.Relu, bias=b1[:, c:c + 1])
                last.then_inc(hid_sb, 1)

            def step(j, at):
                a, b = at(0), at(1)
                if a:
                    relu(a, 0)
                    relu(a, 1)
                    act.wait_ge(gap_done, a.index + 1)
                    nc.scalar.activation(eg[0:n, a.slot, :], gap[0:n, a.slot, :], ACT.Exp)\
                        .then_inc(eg_done, 1)
                if b:
                    act.wait_ge(wtt_ps, b.index + 1)
                    since(act, base_ps, b.index, SL)
                    nc.scalar.activation(wtt[:, b.slot, :], wtt_bank(b.slot), ACT.Copy)\
                        .then_inc(wtt_sb, 1)
                if a:
                    relu(a, 2)
                if b:
                    act.wait_ge(base_ps, b.index + 1)
                    if not (isinstance(b.index, int) and b.index < SL):
                        act.wait_ge(stored[b.slot], (b.index - b.slot) * (16 // SL))
                    nc.scalar.activation(acc[0:n, b.slot, :], base_bank(b.slot), ACT.Copy)\
                        .then_inc(base_sb, 1)
                if a:
                    relu(a, 3)
            pipelined(act, tokens // n, SL, D_, SL, step)

        @block.vector
        def _(dve):
            def step(j, at):
                a = at(0)
                if a:
                    i, sl = a.index, a.slot
                    done = [0]

                    def chained(ins):
                        done[0] += 1
                        ins.then_inc(dstep, 1)
                        dve.wait_ge(dstep, STEPS * i + done[0])

                    dve.wait_ge(l_ps, i + 1)
                    chained(nc.vector.tensor_tensor(logit[0:n, sl, :],
                                                    ps[0:n, 6, 0:E1],
                                                    gate_b[0:n, :], ALU.add))
                    nc.vector.memset(held[:, :], 0.0)
                    chained(nc.vector.max(top[0:n, sl, :], logit[0:n, sl, :]))
                    since(dve, eg_done, i, SL)
                    nc.vector.tensor_tensor(gap[0:n, sl, :], top[0:n, sl, 1:2], top[0:n, sl, 0:1],
                                            ALU.subtract).then_inc(gap_done, 1)
                    chained(nc.vector.max_index(idx[0:n, sl, :], top[0:n, sl, :], logit[0:n, sl, :]))
                    chained(nc.vector.tensor_copy(idf[0:n, sl, :], idx[0:n, sl, 0:2]))
                    dve.wait_ge(eg_done, i + 1)
                    chained(nc.vector.tensor_scalar(ws[0:n, sl, :], eg[0:n, sl, :], 1.0, None, ALU.add))
                    chained(nc.vector.reciprocal(wa[0:n, sl, :], ws[0:n, sl, :]))
                    nc.vector.tensor_scalar(first[0:n, sl, :], expert_ids[0:n, 0:E1], idf[0:n, sl, 0:1],
                                            wa[0:n, sl, :], ALU.is_equal, ALU.mult)
                    chained(nc.vector.tensor_tensor(wb[0:n, sl, :], eg[0:n, sl, :], wa[0:n, sl, :],
                                                    ALU.mult))
                    since(dve, wtt_ps, i, SL)
                    chained(nc.vector.tensor_scalar(wt[0:n, sl, :], expert_ids[0:n, 0:E1],
                                                    idf[0:n, sl, 1:2], wb[0:n, sl, :],
                                                    ALU.is_equal, ALU.mult))
                    nc.vector.tensor_tensor(wt[0:n, sl, :], wt[0:n, sl, :], first[0:n, sl, :],
                                            ALU.add).then_inc(wt_done, 1)
                    assert done[0] == STEPS
                a = at(1)
                if a:
                    i, sl = a.index, a.slot
                    dve.wait_ge(wt_done, i + 1)
                    dve.wait_ge(base_sb, i + 1)
                    for e in range(E1):
                        if e % 4 == 0:
                            dve.wait_ge(y_ps, 2 * i + e // 4 + 1)
                        if e:
                            dve.wait_ge(acc_done, E1 * i + e)
                        nc.vector.scalar_tensor_tensor(
                            out=acc[0:n, sl, :], in0=ps[0:n, 2 + e // 4, (e % 4) * D:(e % 4 + 1) * D],
                            scalar=wt[0:n, sl, e:e + 1], in1=acc[0:n, sl, :],
                            op0=ALU.mult, op1=ALU.add).then_inc(acc_done, 1)
            pipelined(dve, tokens // n, SL, D_, SL, step)


def fold_distance_weights(nc, ps, wt_t, w_out2, w_dist):
    ctx, sb, sem = stage_scope(nc)
    with ctx:
        folded_ps, folded = sem("folded_ps"), sem("folded")
        block = ctx.enter_context(nc.Block())

        @block.tensor
        def _(pe):
            for c in range(CH):
                last = nc.tensor.matmul(ps[:, 0, 0:D], wt_t[:, c, :], w_out2[:, c, :],
                                        start=(c == 0), stop=(c == CH - 1))
            last.then_inc(folded_ps, 1)

        @block.vector
        def _(dve):
            dve.wait_ge(folded_ps, 1)
            nc.vector.tensor_copy(w_dist[:, :], ps[:, 0, 0:D]).then_inc(folded, 1)
            dve.wait_ge(folded, 1)


def vit_tower(nc, A, images, out):
    tokens = images * SEQ
    ctx = ExitStack()
    with ctx:
        ps = ctx.enter_context(nc.psum_tensor("ps", [P, 8, BANK], FP32))
        S = {}
        pairs = []
        for name, (ap, shape) in A.items():
            if name in ("x_main", "x_tail"):
                continue
            S[name] = ctx.enter_context(nc.sbuf_tensor(f"s_{name}", shape,
                                                       BF16 if name in ("before", "all_ones") else FP32))
            pairs.append((S[name][tuple(slice(None) for _ in shape)], ap))
        h = ctx.enter_context(nc.sbuf_tensor("h", [P, tokens], FP32))
        xn = ctx.enter_context(nc.sbuf_tensor("xn", [P, tokens], FP32))
        mean_w = ctx.enter_context(nc.sbuf_tensor("mean_w", [P, P], FP32))
        w_dist = ctx.enter_context(nc.sbuf_tensor("w_dist", [P, D], FP32))

        load_constants(nc, pairs)
        set_mean_weights(nc, mean_w)
        fold_distance_weights(nc, ps, S["a1_wt_t"], S["a1_wout2"], w_dist)
        patch_embed(nc, images, A["x_main"][0], A["x_tail"][0], h, ps, S["w_tok"], S["b_tok"],
                    S["pos"], S["cls"])
        layer_norm(nc, "a0", tokens, h, xn, ps, mean_w)
        attention(nc, "a0", images, h, xn, ps, S["ident"], S["a0_wqkv"], S["a0_wout"], S["a0_bout"],
                  ORDER, b_qk=S["a0_bqk"], b_v=S["a0_bv"][:, :], alphas_raw=S["a0_alphas"][:, :, :])
        layer_norm(nc, "f0", tokens, h, xn, ps, mean_w)
        with nc.sbuf_tensor("gate_all", [P, tokens], FP32) as gate_all:
            route_with_capacity(nc, tokens, xn, ps, S["f0_router"], S["expert_ids"], S["before"],
                                S["all_ones"], S["ident"], gate_all)
            shared_mlp(nc, tokens, h, xn, ps, S["f0_w1"], S["f0_b1"], S["f0_w2"], S["f0_b2"], gate_all)
        layer_norm(nc, "a1", tokens, h, xn, ps, mean_w)
        attention(nc, "a1", images, h, xn, ps, S["ident"], S["a1_wqkv"], S["a1_wout"], S["a1_bout"],
                  1, w_dist=w_dist, dist=S["dist"])
        layer_norm(nc, "f1", tokens, h, xn, ps, mean_w)
        dense_mixture(nc, tokens, h, xn, ps, S["ident"], S["f1_gate"], S["f1_gate_b"], S["expert_ids"],
                      S["f1_w1"], S["f1_b1"], S["f1_w2"], S["f1_b2"], out)


def set_mean_weights(nc, mean_w):
    ctx, sb, sem = stage_scope(nc)
    with ctx:
        mean_w_set = sem("mean_w_set")
        block = ctx.enter_context(nc.Block())

        @block.vector
        def _(dve):
            nc.vector.memset(mean_w[:, :], 1.0 / D).then_inc(mean_w_set, 1)
            dve.wait_ge(mean_w_set, 1)


def kernel(x, L0_tok_W, L0_tok_b, L0_tok_class_token, L0_tok_pos_embed, L0_attn_Wqkv, L0_attn_bqkv,
           L0_attn_Wout, L0_attn_bout, L0_attn_alphas_raw, L0_ffn_router_w, L0_ffn_w1, L0_ffn_b1,
           L0_ffn_w2, L0_ffn_b2, L1_attn_W_qkv, L1_attn_W_out, L1_attn_b_out, L1_ffn_gate_w,
           L1_ffn_gate_b, L1_ffn_w1, L1_ffn_b1, L1_ffn_w2, L1_ffn_b2):
    import math
    import numpy as np
    import ml_dtypes
    import concourse.bacc as bacc
    from concourse.bass_utils import run_bass_kernel_spmd

    a = np.asarray
    images = x.shape[0]
    chunks = images // CHUNK_IMAGES
    n = CHUNK_IMAGES * PATCHES

    def patch_rows(x):
        t = a(x).reshape(chunks, CHUNK_IMAGES, 3, GRID, PATCH, GRID, PATCH)
        return t.transpose(0, 2, 4, 6, 1, 3, 5).reshape(chunks, IN_D, n)
    rows = patch_rows(x)
    w_tok_t = a(L0_tok_W).T
    w_tok = np.zeros((P, KT + 1, D), np.float32)
    w_tok[:, :KT] = w_tok_t[:KT * P].reshape(KT, P, D).transpose(1, 0, 2)
    w_tok[:KR, KT] = w_tok_t[KT * P:]

    def chunk_rows(w):
        return w.reshape(-1, P, w.shape[-1]).transpose(1, 0, 2)

    def repeated(v, rows):
        return np.broadcast_to(a(v)[None], (rows,) + a(v).shape)

    wqkv1 = a(L1_attn_W_qkv)
    wout1 = a(L1_attn_W_out).reshape(H, 2, DH, D)
    place = np.arange(1, SEQ + 1, dtype=np.float32)
    dist = np.exp(-np.abs(place[None, :] - place[:, None]) / np.float32(math.e))
    dist = (dist / dist.sum(-1)).T
    rank = np.arange(P)
    data = {
        "x_main": rows[:, :KT * P].reshape(chunks, KT, P, n).transpose(0, 2, 1, 3),
        "x_tail": rows[:, KT * P:],
        "w_tok": w_tok,
        "b_tok": a(L0_tok_b)[:, None],
        "pos": a(L0_tok_pos_embed).T,
        "cls": a(L0_tok_class_token).T,
        "a0_wqkv": a(L0_attn_Wqkv),
        "a0_bqk": a(L0_attn_bqkv)[:2 * INNER].reshape(2 * CH, P).T,
        "a0_bv": repeated(a(L0_attn_bqkv)[2 * INNER:], SEQ),
        "a0_wout": chunk_rows(a(L0_attn_Wout)),
        "a0_bout": a(L0_attn_bout)[:, None],
        "a0_alphas": repeated(L0_attn_alphas_raw, SEQ),
        "f0_router": a(L0_ffn_router_w).T,
        "f0_w1": a(L0_ffn_w1).T,
        "f0_b1": a(L0_ffn_b1).reshape(F0 // P, P).T,
        "f0_w2": chunk_rows(a(L0_ffn_w2).T),
        "f0_b2": a(L0_ffn_b2)[:, None],
        "a1_wqkv": wqkv1[:, :3 * INNER],
        "a1_wt_t": chunk_rows(wqkv1[:, 3 * INNER:].T),
        "a1_wout": chunk_rows(wout1[:, 0].reshape(INNER, D)),
        "a1_wout2": chunk_rows(wout1[:, 1].reshape(INNER, D)),
        "a1_bout": a(L1_attn_b_out)[:, None],
        "f1_gate": a(L1_ffn_gate_w),
        "f1_gate_b": repeated(L1_ffn_gate_b, P),
        "f1_w1": a(L1_ffn_w1).transpose(1, 0, 2).reshape(D, E1 * F1),
        "f1_b1": a(L1_ffn_b1).reshape(E1 * F1 // P, P).T,
        "f1_w2": chunk_rows(a(L1_ffn_w2).reshape(E1 * F1, D)),
        "f1_b2": a(L1_ffn_b2),
        "ident": np.eye(P, dtype=np.float32),
        "dist": dist.astype(np.float32),
        "expert_ids": np.tile(np.arange(E0, dtype=np.float32), (P, 1)),
        "before": (rank[:, None] < rank[None, :]).astype(ml_dtypes.bfloat16),
        "all_ones": np.ones((P, P), ml_dtypes.bfloat16),
    }
    nc = bacc.Bacc("TRN2", target_bir_lowering=False, num_devices=1)
    arrays, A = {}, {}
    for name, v in data.items():
        v = np.ascontiguousarray(v)
        arrays[f"in_{name}"] = v
        ap = nc.dram_tensor(f"in_{name}", v.shape, mybir.dt.from_np(v.dtype), kind="ExternalInput").ap()
        A[name] = (ap, list(v.shape))
    out = nc.dram_tensor("out", (images * SEQ, D), FP32, kind="ExternalOutput").ap()
    vit_tower(nc, A, images, out)
    r = run_bass_kernel_spmd(nc, [arrays], core_ids=[0])
    return r.results[0]["out"].reshape(images, SEQ, D)
```

```python
import concourse.bass as bass
from concourse import mybir
from contextlib import ExitStack

FP32 = mybir.dt.float32
U32 = mybir.dt.uint32
BF16 = mybir.dt.bfloat16
ALU = mybir.AluOpType
ACT = mybir.ActivationFunctionType
AX = mybir.AxisListType

P = 128
D = 128
GRID = 8
PATCHES = GRID * GRID
SEQ = PATCHES + 1
PATCH = 28
IN_D = 3 * PATCH * PATCH
KT = IN_D // P
KR = IN_D - KT * P
H, DH = 8, 64
INNER = H * DH
CH = INNER // P
SCALE = DH ** -0.5
ORDER = 3
E0, E1 = 64, 8
CAPACITY = 128
F0, F1 = 512, 256
EPS = 1e-5
BANK = 512
CHUNK_IMAGES = 8


class At:

    def __init__(self, index, slot):
        self.index, self.slot = index, slot


def pipelined(eng, items, unroll, depth, lag, step):
    groups, lead = items // unroll, -(-(depth + lag) // unroll)
    assert lead < groups

    def group(g, fixed):
        for j in range(unroll):
            def at(s, j=j):
                slot = (j - s) % unroll
                if fixed:
                    i = g * unroll + j - s
                    return At(i, slot) if 0 <= i < items else None
                return At(g * unroll + (j - s), slot)
            step(j, at)

    for g in range(lead):
        group(g, True)
    with eng.Fori(lead, groups) as g:
        group(g, False)
    for g in range(groups, -(-(items + depth) // unroll)):
        group(g, True)


def stage_scope(nc):
    ctx = ExitStack()

    def sb(name, shape, dt=FP32):
        return ctx.enter_context(nc.sbuf_tensor(name, shape, dt))

    def sem(name):
        return ctx.enter_context(nc.semaphore(name))

    return ctx, sb, sem


def patch_embed(nc, images, x_main, x_tail, h, ps, w_tok, b_tok, pos, cls, own_loads, later_loads):
    n = CHUNK_IMAGES * PATCHES
    chunks = images // CHUNK_IMAGES
    pieces = 3
    kp = KT // pieces
    ctx, sb, sem = stage_scope(nc)
    with ctx:
        xb = sb("x_chunk", [P, 2, KT + 1, n])
        x_in = [[sem(f"x_in_{s}_{i}") for i in range(pieces)] for s in range(2)]
        tok_ps = sem("tok_ps")
        tok_done = sem("tok_done")
        cls_done = sem("cls_done")
        own_loaded, later_loaded = sem("own_loaded"), sem("later_loaded")
        block = ctx.enter_context(nc.Block())

        @block.scalar
        def _(act):
            for dst, src in own_loads:
                act.dma_start(dst, src).then_inc(own_loaded, 16)
            act.wait_ge(own_loaded, 16 * len(own_loads))
            for dst, src in later_loads:
                act.dma_start(dst, src).then_inc(later_loaded, 16)
            act.wait_ge(later_loaded, 16 * len(later_loads))

        @block.sync
        def _(sp):
            def step(j, at):
                a = at(0)
                if a:
                    if not (isinstance(a.index, int) and a.index < 2):
                        sp.wait_ge(tok_ps, a.index - 1)
                    for i in range(pieces):
                        sp.dma_start(xb[:, a.slot, i * kp:(i + 1) * kp, :],
                                     x_main[bass.ds(a.index, 1), :, i * kp:(i + 1) * kp, :]
                                     .rearrange("o p k n -> (o p) k n")).then_inc(x_in[a.slot][i], 16)
                    sp.dma_start(xb[0:KR, a.slot, KT, :],
                                 x_tail[bass.ds(a.index, 1), :, :]
                                 .rearrange("o p n -> (o p) n")).then_inc(x_in[a.slot][pieces - 1], 16)
            pipelined(sp, chunks, 2, 0, 2, step)

        @block.tensor
        def _(pe):
            pe.wait_ge(own_loaded, 16 * len(own_loads))

            def step(j, at):
                a = at(0)
                if a:
                    loads = (a.index - a.slot) // 2 + 1 if isinstance(a.index, int) else None
                    if not (isinstance(a.index, int) and a.index < 2):
                        pe.wait_ge(tok_done, a.index - 1)
                    for i in range(pieces):
                        per = 32 if i == pieces - 1 else 16
                        if loads is not None:
                            pe.wait_ge(x_in[a.slot][i], per * loads)
                        else:
                            pe.wait_ge(x_in[a.slot][i], (a.index - a.slot) * (per // 2) + per)
                        for k in range(i * kp, (i + 1) * kp):
                            nc.tensor.matmul(ps[:, a.slot, :], w_tok[:, k, :], xb[:, a.slot, k, :],
                                             start=(k == 0), stop=False)
                    nc.tensor.matmul(ps[:, a.slot, :], w_tok[0:KR, KT, :], xb[0:KR, a.slot, KT, :],
                                     start=False, stop=True).then_inc(tok_ps, 1)
            pipelined(pe, chunks, 2, 0, 2, step)

        @block.vector
        def _(dve):
            hv = h[:, :].rearrange("p (b t) -> p b t", t=SEQ)
            dve.wait_ge(own_loaded, 16 * len(own_loads))
            nc.vector.tensor_scalar(hv[:, :, 0], pos[:, 0:1].to_broadcast([P, images]), cls[:, 0:1],
                                    None, ALU.mult).then_inc(cls_done, 1)

            def step(j, at):
                a = at(0)
                if a:
                    dve.wait_ge(tok_ps, a.index + 1)
                    out = h[:, bass.ds(a.index * (CHUNK_IMAGES * SEQ), CHUNK_IMAGES * SEQ)]\
                        .rearrange("p (b t) -> p b t", t=SEQ)[:, :, 1:SEQ]
                    nc.vector.scalar_tensor_tensor(
                        out=out, in0=ps[:, a.slot, :].rearrange("p (b t) -> p b t", t=PATCHES),
                        scalar=b_tok[:, 0:1],
                        in1=pos[:, 1:SEQ].unsqueeze(1).to_broadcast([P, CHUNK_IMAGES, PATCHES]),
                        op0=ALU.add, op1=ALU.mult).then_inc(tok_done, 1)
            pipelined(dve, chunks, 2, 0, 2, step)


def layer_norm(nc, tag, tokens, h, xn, ps, mean_w, spread_w):
    n = 260
    Q = 4
    QP = P // Q
    groups = tokens // (Q * n)
    assert groups * Q * n == tokens
    ctx, sb, sem = stage_scope(nc)
    with ctx:
        xc = sb(f"centered_{tag}", [P, 2, Q, n])
        sq = sb(f"squared_{tag}", [P, 2, Q, n])
        sd = sb(f"deviation_{tag}", [P, 2, n])
        rstd = sb(f"rstd_{tag}", [P, 2, n])
        eps = sb(f"eps_{tag}", [P, 1])
        eps_set = sem(f"eps_set_{tag}")
        mean_ps, centered = sem(f"mean_ps_{tag}"), sem(f"centered_{tag}_s")
        squared, var_ps = sem(f"squared_{tag}_s"), sem(f"var_ps_{tag}")
        sd_done, rstd_done = sem(f"sd_done_{tag}"), sem(f"rstd_done_{tag}")
        spread_ps, normed = sem(f"spread_ps_{tag}"), sem(f"normed_{tag}")
        block = ctx.enter_context(nc.Block())

        def cols(t, a, i):
            return t[:, bass.ds(a.index * (Q * n) + i * n, n)]

        def since(eng, sm, index, lag):
            if not (isinstance(index, int) and index < lag):
                eng.wait_ge(sm, index - lag + 1)

        @block.tensor
        def _(pe):
            def step(j, at):
                a = at(2)
                if a:
                    pe.wait_ge(rstd_done, a.index + 1)
                    for i in range(Q):
                        if i >= 2 or not (isinstance(a.index, int) and a.index < 1):
                            pe.wait_ge(normed, Q * a.index + i - 1)
                        rows = slice(i * QP, (i + 1) * QP)
                        nc.tensor.matmul(ps[:, 6 + i % 2, 0:n], spread_w[rows, :], rstd[rows, a.slot, :],
                                         start=True, stop=True).then_inc(spread_ps, 1)
                a = at(1)
                if a:
                    pe.wait_ge(squared, a.index + 1)
                    since(pe, sd_done, a.index, 2)
                    for i in range(Q):
                        last = nc.tensor.matmul(ps[i * QP:(i + 1) * QP, 4 + a.slot, 0:n],
                                                mean_w[:, 0:QP], sq[:, a.slot, i, :],
                                                start=True, stop=True)
                    last.then_inc(var_ps, 1)
                a = at(0)
                if a:
                    for i in range(Q):
                        if not (isinstance(a.index, int) and a.index < 1):
                            pe.wait_ge(centered, Q * a.index - Q + i + 1)
                        nc.tensor.matmul(ps[:, i, 0:n], mean_w[:, :], cols(h, a, i),
                                         start=True, stop=True).then_inc(mean_ps, 1)
            pipelined(pe, groups, 2, 2, 2, step)

        @block.scalar
        def _(act):
            act.wait_ge(eps_set, 1)

            def step(j, at):
                a = at(1)
                if a:
                    act.wait_ge(var_ps, a.index + 1)
                    since(act, rstd_done, a.index, 2)
                    nc.scalar.activation(sd[:, a.slot, :], ps[:, 4 + a.slot, 0:n], ACT.Sqrt,
                                         bias=eps[:, 0:1]).then_inc(sd_done, 1)
                a = at(0)
                if a:
                    act.wait_ge(centered, Q * a.index + Q)
                    since(act, var_ps, a.index, 2)
                    nc.scalar.activation(sq[:, a.slot, :, :], xc[:, a.slot, :, :], ACT.Square)\
                        .then_inc(squared, 1)
            pipelined(act, groups, 2, 2, 2, step)

        @block.vector
        def _(dve):
            nc.vector.memset(eps[:, :], EPS).then_inc(eps_set, 1)

            def step(j, at):
                a = at(2)
                if a:
                    for i in range(Q):
                        dve.wait_ge(spread_ps, Q * a.index + i + 1)
                        nc.vector.tensor_tensor(cols(xn, a, i), xc[:, a.slot, i, :],
                                                ps[:, 6 + i % 2, 0:n], ALU.mult).then_inc(normed, 1)
                a = at(1)
                if a:
                    dve.wait_ge(sd_done, a.index + 1)
                    if not (isinstance(a.index, int) and a.index < 2):
                        dve.wait_ge(spread_ps, Q * a.index - Q)
                    nc.vector.reciprocal(rstd[:, a.slot, :], sd[:, a.slot, :]).then_inc(rstd_done, 1)
                a = at(0)
                if a:
                    since(dve, squared, a.index, 2)
                    if not (isinstance(a.index, int) and a.index < 2):
                        dve.wait_ge(normed, Q * a.index - Q)
                    for i in range(Q):
                        dve.wait_ge(mean_ps, Q * a.index + i + 1)
                        nc.vector.tensor_tensor(xc[:, a.slot, i, :], cols(h, a, i), ps[:, i, 0:n],
                                                ALU.subtract).then_inc(centered, 1)
            pipelined(dve, groups, 2, 2, 2, step)


def attention(nc, tag, images, h, xn, ps, ident, w_qkv, w_out, b_out, order, b_qk=None,
              alphas=None, w_dist=None, dist=None):
    masked = order > 1
    TS = 3
    RS = 4
    XS = RS + order
    OS = XS + 2 + XS % 2
    PAIR = 2 * SEQ
    DROP = 1e30
    ctx, sb, sem = stage_scope(nc)
    with ctx:
        xs = sb(f"xn_images_{tag}", [P, 4, SEQ])
        qk = sb(f"qk_{tag}", [P, 2, 2 * CH, PAIR])
        v = sb(f"v_{tag}", [SEQ, 4, H, DH + 1])
        neg_s = sb(f"neg_scores_{tag}", [SEQ, 2, 2, CH, SEQ])
        below = sb(f"below_max_{tag}", [SEQ, 2, 2, CH, SEQ])
        e = sb(f"e_{tag}", [SEQ, 2, 2, CH, SEQ])
        neg_max = sb(f"neg_max_{tag}", [SEQ, 2, 2, CH])
        et = sb(f"eT_{tag}", [SEQ, 4, 2, CH, SEQ])
        inv = sb(f"inv_sum_{tag}", [SEQ, 4, H])
        res = sb(f"res_{tag}", [SEQ, 2, INNER])
        res_t = sb(f"resT_{tag}", [P, 2, CH, PAIR])
        if masked:
            low8 = sb(f"low8_{tag}", [SEQ, 2, 2, CH, 8])
            drop = sb(f"drop_{tag}", [SEQ, 2, 2, CH, SEQ])
            far = sb(f"below_masked_{tag}", [SEQ, 2, 2, CH, SEQ])
            inv_a = sb(f"inv_sum_alpha_{tag}", [SEQ, 2, H])
            va = sb(f"v_alpha_{tag}", [SEQ, 2, 4, H, DH])
            tv = sb(f"Av_{tag}", [SEQ, 2, 2, H, DH])
            cv = sb(f"horner_{tag}", [SEQ, 2, 2, H, DH])
        else:
            far = below
            wv = sb(f"dist_values_{tag}", [SEQ, 4, D])

        def s(name):
            return sem(f"{name}_{tag}")
        ones_set = s("ones_set")
        xs_copied = s("xs_copied")
        qk_ps, qk_sb = s("qk_ps"), s("qk_sb")
        v_ps, v_sb = s("v_ps"), s("v_sb")
        s_ps, neg_done, max_done, below_done = s("s_ps"), s("neg_done"), s("max_done"), s("below_done")
        exp_done = s("exp_done")
        t_ps, et_sb = s("t_ps"), s("et_sb")
        inv_done = s("inv_done")
        r_ps = [s(f"r{n}_ps") for n in range(order)]
        r_sb = [s(f"r{n}_sb") for n in range(order)]
        x_ps, x_sb = s("x_ps"), s("x_sb")
        if masked:
            va_done, low_done, drop_done, inv_a_done = (s("va_done"), s("low_done"), s("drop_done"),
                                                        s("inv_a_done"))
            far_done = s("far_done")
            c_done = [s(f"c{n}_done") for n in range(2)]
        else:
            far_done = below_done
            w_ps, w_sb = s("w_ps"), s("w_sb")
            d_ps, d_added = s("d_ps"), s("d_added")
        o_ps, o_added = s("o_ps"), s("o_added")
        block = ctx.enter_context(nc.Block())

        def since(eng, sm, index, lag, more=0):
            if not (isinstance(index, int) and index < lag):
                eng.wait_ge(sm, index - lag + 1 + more)

        def natural(t):
            return t.rearrange("p (c b) d -> p b c d", b=2)

        def over_d(t):
            return t.unsqueeze(2).to_broadcast([SEQ, H, DH])

        def over_keys(t):
            return t.unsqueeze(3).to_broadcast([SEQ, 2, CH, SEQ])

        @block.gpsimd
        def _(pool):
            nc.gpsimd.memset(v[:, :, :, DH:DH + 1], 1.0).then_inc(ones_set, 1)

            def step(j, at):
                a = at(0)
                if a and j % 2 == 0:
                    since(pool, v_ps, a.index, 4, 1)
                    if not masked:
                        since(pool, w_ps, a.index, 4, 1)
                    nc.gpsimd.tensor_copy(xs[:, a.slot:a.slot + 2, :].rearrange("p a t -> p (a t)"),
                                          xn[:, bass.ds(a.index * SEQ, PAIR)]).then_inc(xs_copied, 2)
                if not masked:
                    return
                a = at(RS)
                if a:
                    pool.wait_ge(r_sb[0], a.index + 1)
                    since(pool, r_ps[1], a.index, 2)
                    nc.gpsimd.tensor_tensor(cv[:, 0, a.slot % 2], tv[:, 0, a.slot % 2],
                                            va[:, 1, a.slot], ALU.add).then_inc(c_done[0], 1)
                a = at(RS + 1)
                if a:
                    pool.wait_ge(r_sb[1], a.index + 1)
                    since(pool, r_ps[2], a.index, 2)
                    nc.gpsimd.tensor_tensor(cv[:, 1, a.slot % 2], tv[:, 1, a.slot % 2],
                                            va[:, 0, a.slot], ALU.add).then_inc(c_done[1], 1)
                a = at(2)
                if a:
                    pool.wait_ge(v_sb, a.index + 1)
                    since(pool, c_done[1], a.index, 4)
                    for n in range(2):
                        nc.gpsimd.tensor_tensor(va[:, n, a.slot], v[:, a.slot, :, 0:DH],
                                                over_d(alphas[:, n, :]), ALU.mult).then_inc(va_done, 1)
                    pool.wait_ge(va_done, 2 * a.index + 2)
            pipelined(pool, images, 4, OS, 4, step)

        @block.scalar
        def _(act):
            act.wait_ge(ones_set, 1)

            def qk_out(a, m):
                act.wait_ge(qk_ps, 2 * a.index + m + 1)
                if m == 0:
                    since(act, s_ps, a.index, 4, 1)
                for n, c in enumerate((m, CH + m)):
                    last = nc.scalar.activation(
                        qk[:, a.slot // 2, c, :], ps[:, 4 + m % 2, n * PAIR:(n + 1) * PAIR],
                        ACT.Identity, bias=b_qk[:, c:c + 1] if b_qk is not None else 0.0)
                last.then_inc(qk_sb, 1)

            def step(j, at):
                a = at(2)
                if a:
                    if not masked:
                        act.wait_ge(w_ps, a.index + 1)
                        since(act, d_ps, a.index - a.slot % 2, 4, 1)
                        nc.scalar.activation(wv[:, a.slot], ps[0:SEQ, 3, BANK - D:BANK], ACT.Copy)\
                            .then_inc(w_sb, 1)
                    act.wait_ge(v_ps, a.index + 1)
                    since(act, r_ps[0], a.index, 4)
                    if masked:
                        since(act, va_done, a.index, 4, a.index - 3)
                    nc.scalar.activation(v[:, a.slot, :, 0:DH],
                                         ps[0:SEQ, 4, :].rearrange("p (h d) -> p h d", d=DH),
                                         ACT.Copy).then_inc(v_sb, 1)
                a = at(XS)
                if a:
                    act.wait_ge(x_ps, a.index + 1)
                    since(act, o_ps, a.index - a.slot % 2, 4, 1)
                    nc.scalar.activation(
                        res_t[:, a.slot // 2, :, (a.slot % 2) * SEQ:(a.slot % 2 + 1) * SEQ],
                        ps[:, 5, 0:CH * SEQ].rearrange("p (c q) -> p c q", q=SEQ), ACT.Copy)\
                        .then_inc(x_sb, 1)
                a = at(TS)
                if a:
                    act.wait_ge(t_ps, a.index + 1)
                    since(act, r_ps[-1], a.index, 4)
                    nc.scalar.activation(
                        et[:, a.slot], ps[0:SEQ, 2:4, 0:CH * SEQ].rearrange("p b (c k) -> p b c k", k=SEQ),
                        ACT.Copy).then_inc(et_sb, 1)
                a = at(0)
                if a and j % 2 == 0:
                    qk_out(a, 0)
                    qk_out(a, 1)
                a = at(1)
                if a:
                    act.wait_ge(s_ps, a.index + 1)
                    since(act, far_done, a.index, 2)
                    nc.scalar.activation(neg_s[:, a.slot % 2],
                                         ps[0:SEQ, 0:2, 0:CH * SEQ]
                                         .rearrange("p b (c k) -> p b c k", k=SEQ),
                                         ACT.Copy, scale=-1.0).then_inc(neg_done, 1)
                a = at(0)
                if a and j % 2 == 0:
                    qk_out(a, 2)
                    qk_out(a, 3)
                a = at(2)
                if a:
                    act.wait_ge(far_done, a.index + 1)
                    since(act, t_ps, a.index, 2)
                    nc.scalar.activation(e[:, a.slot % 2], far[:, a.slot % 2], ACT.Exp, scale=-SCALE)\
                        .then_inc(exp_done, 1)
            pipelined(act, images, 4, OS, 4, step)

        @block.vector
        def _(dve):
            def read_out(n, a, factor):
                dve.wait_ge(r_ps[n], a.index + 1)
                if n < order - 1:
                    since(dve, c_done[n], a.index, 2)
                    dst = tv[:, n, a.slot % 2]
                else:
                    since(dve, x_ps, a.index, 2)
                    dst = res[:, a.slot % 2].rearrange("p (h d) -> p h d", d=DH)
                if n == 0:
                    src = ps[0:SEQ, 6:8, 0:CH * (DH + 1)]\
                        .rearrange("p b (c d) -> p b c d", d=DH + 1)[:, :, :, 0:DH]
                    last = nc.vector.tensor_tensor(natural(dst), src, natural(over_d(factor)), ALU.mult)
                else:
                    src = ps[0:SEQ, 5 + n, :].rearrange("p (h d) -> p h d", d=DH)
                    last = nc.vector.tensor_tensor(dst, src, over_d(factor), ALU.mult)
                last.then_inc(r_sb[n], 1)

            def step(j, at):
                even = j % 2 == 0
                a = at(RS)
                if a:
                    dve.wait_ge(r_ps[0], a.index + 1)
                    nc.vector.reciprocal(
                        inv[:, a.slot, :].rearrange("p (c b) -> p b c", b=2),
                        ps[0:SEQ, 6:8, 0:CH * (DH + 1)]
                        .rearrange("p b (c d) -> p b c d", d=DH + 1)[:, :, :, DH]).then_inc(inv_done, 1)
                    dve.wait_ge(inv_done, a.index + 1)
                    if masked:
                        nc.vector.tensor_tensor(inv_a[:, a.slot % 2, :], inv[:, a.slot, :],
                                                alphas[:, ORDER - 1, :], ALU.mult).then_inc(inv_a_done, 1)
                        dve.wait_ge(inv_a_done, a.index + 1)
                        read_out(0, a, inv_a[:, a.slot % 2, :])
                    else:
                        read_out(0, a, inv[:, a.slot, :])
                if a and even and not masked:
                    dve.wait_ge(d_ps, a.index + 2)
                    hp = h[:, bass.ds(a.index * SEQ, PAIR)]
                    nc.vector.tensor_tensor(hp, hp, ps[:, 6, BANK - PAIR:BANK], ALU.add)\
                        .then_inc(d_added, 2)
                a = at(2)
                if a:
                    sl = a.slot % 2
                    dve.wait_ge(neg_done, a.index + 1)
                    nc.vector.tensor_reduce(neg_max[:, sl], neg_s[:, sl], AX.X, ALU.min)\
                        .then_inc(max_done, 1)
                    dve.wait_ge(max_done, a.index + 1)
                    since(dve, exp_done, a.index, 2)
                    nc.vector.tensor_tensor(below[:, sl], neg_s[:, sl], over_keys(neg_max[:, sl]),
                                            ALU.subtract).then_inc(below_done, 1)
                p = at(OS)
                if p and even:
                    dve.wait_ge(o_ps, p.index + 2)
                    hp = h[:, bass.ds(p.index * SEQ, PAIR)]
                    nc.vector.scalar_tensor_tensor(out=hp, in0=ps[:, 1, BANK - PAIR:BANK], scalar=b_out[:, 0:1],
                                                   in1=hp, op0=ALU.add, op1=ALU.add).then_inc(o_added, 2)
                if not masked:
                    return
                b = at(RS + 1)
                if b:
                    read_out(1, b, inv[:, b.slot, :])
                b = at(RS + 2)
                if b:
                    read_out(2, b, inv[:, b.slot, :])
                if a:
                    for b in range(2):
                        for c in range(CH):
                            last = nc.vector.max(low8[:, sl, b, c, :], neg_s[:, sl, b, c, :])
                    last.then_inc(low_done, 1)
                    dve.wait_ge(low_done, a.index + 1)
                    nc.vector.tensor_tensor(drop[:, sl], neg_s[:, sl], over_keys(low8[:, sl, :, :, 1]),
                                            ALU.is_gt).then_inc(drop_done, 1)
                    dve.wait_ge(drop_done, a.index + 1)
                    nc.vector.scalar_tensor_tensor(out=far[:, sl], in0=drop[:, sl], scalar=DROP,
                                                   in1=below[:, sl], op0=ALU.mult, op1=ALU.add)\
                        .then_inc(far_done, 1)
            pipelined(dve, images, 4, OS, 4, step)

        @block.tensor
        def _(pe):
            def project_qk(a, m, at):
                pe.wait_ge(xs_copied, a.index + 2)
                if m == 0:
                    if at(2):
                        pe.wait_ge(v_sb, at(2).index + 1)
                elif m == 1:
                    if at(XS):
                        pe.wait_ge(x_sb, at(XS).index + 1)
                    elif not (isinstance(a.index, int) and a.index < 2):
                        pe.wait_ge(qk_sb, 2 * a.index)
                else:
                    pe.wait_ge(qk_sb, 2 * a.index + m - 1)
                for n, c in enumerate((m, CH + m)):
                    last = nc.tensor.matmul(ps[:, 4 + m % 2, n * PAIR:(n + 1) * PAIR],
                                            w_qkv[:, c * P:(c + 1) * P],
                                            xs[:, a.slot:a.slot + 2, :].rearrange("p a t -> p (a t)"),
                                            start=True, stop=True)
                last.then_inc(qk_ps, 1)

            def project_out(at):
                a = at(OS)
                if a and a.slot % 2 == 0:
                    pe.wait_ge(x_sb, a.index + 2)
                    if at(2):
                        pe.wait_ge(neg_done, at(2).index + 1)
                    if not (isinstance(a.index, int) and a.index < 2):
                        pe.wait_ge(o_added, a.index)
                    for c in range(CH):
                        last = nc.tensor.matmul(ps[:, 1, BANK - PAIR:BANK], w_out[:, c, :],
                                                res_t[:, a.slot // 2, c, :],
                                                start=(c == 0), stop=(c == CH - 1))
                    last.then_inc(o_ps, 2)

            def product(n, a):
                for hd in range(H):
                    c, b = hd // 2, hd % 2
                    if n == 0:
                        out = ps[0:SEQ, 6 + b, c * (DH + 1):(c + 1) * (DH + 1)]
                        rhs = v[:, a.slot, hd, :]
                    else:
                        out = ps[0:SEQ, 5 + n, hd * DH:(hd + 1) * DH]
                        rhs = cv[:, n - 1, a.slot % 2, hd, :]
                    last = nc.tensor.matmul(out, et[:, a.slot, b, c, :], rhs, start=True, stop=True)
                last.then_inc(r_ps[n], 1)

            def step(j, at):
                even = j % 2 == 0
                a = at(RS)
                if a:
                    pe.wait_ge(et_sb, a.index + 1)
                    pe.wait_ge(v_sb, a.index + 1)
                    since(pe, r_sb[0], a.index, 1)
                    if masked:
                        since(pe, r_sb[1], a.index, 2)
                        since(pe, r_sb[2], a.index, 3)
                    elif not even:
                        pe.wait_ge(d_added, a.index + 1)
                    elif not (isinstance(a.index, int) and a.index < 2):
                        pe.wait_ge(d_added, a.index)
                    if even and not masked:
                        pe.wait_ge(w_sb, a.index + 2)
                        for n in range(2):
                            last = nc.tensor.matmul(ps[:, 6, BANK - PAIR + n * SEQ:BANK - PAIR + (n + 1) * SEQ],
                                                    wv[:, a.slot + n, :], dist[0:SEQ, :],
                                                    start=True, stop=True)
                        last.then_inc(d_ps, 2)
                    product(0, a)
                if masked:
                    project_out(at)
                a = at(2)
                if a:
                    if not masked:
                        since(pe, w_sb, a.index, 1)
                        since(pe, et_sb, a.index, 2)
                        nc.tensor.matmul(ps[0:SEQ, 3, BANK - D:BANK], xs[:, a.slot, :], w_dist[:, :],
                                         start=True, stop=True).then_inc(w_ps, 1)
                    if not even and at(1):
                        pe.wait_ge(qk_sb, 2 * at(1).index + 3)
                    else:
                        since(pe, v_sb, a.index, 1)
                    nc.tensor.matmul(ps[0:SEQ, 4, :], xs[:, a.slot, :], w_qkv[:, 2 * INNER:3 * INNER],
                                     start=True, stop=True).then_inc(v_ps, 1)
                if not masked:
                    project_out(at)
                a = at(XS)
                if a:
                    pe.wait_ge(r_sb[-1], a.index + 1)
                    if not even and at(1):
                        pe.wait_ge(qk_sb, 2 * at(1).index + 4)
                    else:
                        since(pe, x_sb, a.index, 1)
                    for c in range(CH):
                        last = nc.tensor.transpose(ps[:, 5, c * SEQ:(c + 1) * SEQ],
                                                   res[:, a.slot % 2, c * P:(c + 1) * P],
                                                   ident[0:SEQ, 0:SEQ])
                    last.then_inc(x_ps, 1)
                a = at(TS)
                if a:
                    pe.wait_ge(exp_done, a.index + 1)
                    since(pe, et_sb, a.index, 1)
                    if not masked and at(2):
                        pe.wait_ge(w_sb, at(2).index + 1)
                    for b in range(2):
                        for c in range(CH):
                            last = nc.tensor.transpose(ps[0:SEQ, 2 + b, c * SEQ:(c + 1) * SEQ],
                                                       e[:, a.slot % 2, b, c, :], ident[0:SEQ, 0:SEQ])
                    last.then_inc(t_ps, 1)
                a = at(RS + 1)
                if a and masked:
                    pe.wait_ge(c_done[0], a.index + 1)
                    if at(RS):
                        pe.wait_ge(r_sb[0], at(RS).index + 1)
                    else:
                        since(pe, r_sb[1], a.index, 1)
                    product(1, a)
                a = at(RS + 2)
                if a and masked:
                    pe.wait_ge(c_done[1], a.index + 1)
                    if not at(RS):
                        since(pe, r_sb[2], a.index, 1)
                    product(2, a)
                a = at(0)
                if a and even:
                    project_qk(a, 0, at)
                    project_qk(a, 1, at)
                a = at(1)
                if a:
                    pe.wait_ge(qk_sb, 2 * (a.index - a.slot % 2) + 4)
                    since(pe, neg_done, a.index, 1)
                    if even and at(OS):
                        pe.wait_ge(o_added, at(OS).index + 2)
                    for hd in range(H):
                        c, b = hd // 2, hd % 2
                        rows = slice(b * DH, (b + 1) * DH)
                        cols = slice((a.slot % 2) * SEQ, (a.slot % 2 + 1) * SEQ)
                        last = nc.tensor.matmul(ps[0:SEQ, b, c * SEQ:(c + 1) * SEQ],
                                                qk[rows, a.slot // 2, c, cols],
                                                qk[rows, a.slot // 2, CH + c, cols],
                                                start=True, stop=True)
                    last.then_inc(s_ps, 1)
                a = at(0)
                if a and even:
                    project_qk(a, 2, at)
                    project_qk(a, 3, at)
            pipelined(pe, images, 4, OS, 4, step)


def route_with_capacity(nc, tokens, xn, ps, router, expert_ids, before, all_ones, ident, gate_all):
    T = 5
    groups = tokens // (T * P)
    assert groups * T * P == tokens
    ctx, sb, sem = stage_scope(nc)
    with ctx:
        xs = sb("xn_tiles_r", [P, 2, T * P])
        held = sb("held_r", [P, 1])
        top = sb("top8_r", [P, 2, T, 8])
        idx = sb("index8_r", [P, 2, T, 8], U32)
        idf = sb("index_r", [P, 2, T, 2])
        below = sb("below_max_r", [P, 2, T, E0])
        prob = sb("prob_r", [P, 2, T, E0])
        total = sb("prob_sum_r", [P, 2, T])
        inv = sb("inv_sum_r", [P, 2, T])
        first = sb("first_choice", [P, 2, T, E0])
        second = sb("second_choice", [P, 2, T, E0])
        both = sb("both_choices", [P, 2, T, E0], BF16)
        count = sb("count_before", [P, 2, T, E0])
        carry = sb("count_carry", [P, E0])
        kept = sb("kept_choice", [P, 2, T, E0])
        terms = sb("gate_terms", [P, 2, T, E0])
        gsum = sb("gate_sum", [P, 2, T])
        gate = sb("gate_r", [P, 2, T])
        gate_w = sb("gate_wide", [P, 2, T, P])
        copied, l_ps = sem("xs_copied_r"), sem("logits_ps_r")
        top_done, idx_done, idf_done = sem("top_done_r"), sem("idx_done_r"), sem("idf_done_r")
        below_done, prob_done = sem("below_done_r"), sem("prob_done_r")
        choice_done, both_done = sem("choice_done_r"), sem("both_done_r")
        rank_ps, carry_set, carry_done = sem("rank_ps_r"), sem("carry_set_r"), sem("carry_done_r")
        count_done, kept_done, terms_done = sem("count_done_r"), sem("kept_done_r"), sem("terms_r")
        sum_done, total_done = sem("gate_sum_r_s"), sem("total_done_r")
        inv_done, gate_done, wide_done = sem("inv_done_r"), sem("gate_done_r"), sem("wide_done_r")
        bc_ps, bc_done = sem("gate_ps_r"), sem("gate_all_done_r")
        block = ctx.enter_context(nc.Block())
        PARTS = ((0, 3), (3, T))

        def since(eng, sm, index, lag, per=1):
            if not (isinstance(index, int) and index < lag):
                eng.wait_ge(sm, index * per - (lag - 1) * per)

        def logits(slot):
            return ps[:, slot, 0:T * E0].rearrange("p (t e) -> p t e", e=E0)

        def places(slot):
            return ps[:, 2 + slot, 0:(T + 1) * E0].rearrange("p (t e) -> p t e", e=E0)

        def each_expert(t):
            return t.unsqueeze(2).to_broadcast([P, T, E0])

        def each_tile(t):
            return t.unsqueeze(1).to_broadcast([P, T, E0])

        @block.gpsimd
        def _(pool):
            def step(j, at):
                a = at(0)
                if a:
                    since(pool, l_ps, a.index, 2)
                    nc.gpsimd.tensor_copy(xs[:, a.slot, :], xn[:, bass.ds(a.index * (T * P), T * P)])\
                        .then_inc(copied, 1)
            pipelined(pool, groups, 2, 2, 2, step)

        @block.tensor
        def _(pe):
            def step(j, at):
                a = at(0)
                if a:
                    pe.wait_ge(copied, a.index + 1)
                    since(pe, below_done, a.index, 2)
                    since(pe, idx_done, a.index, 2)
                    for t in range(T):
                        last = nc.tensor.matmul(logits(a.slot)[:, t, :], xs[:, a.slot, t * P:(t + 1) * P],
                                                router[:, :], start=True, stop=True)
                    last.then_inc(l_ps, 1)
                a = at(1)
                if a:
                    pe.wait_ge(both_done, a.index + 1)
                    since(pe, carry_done, a.index, 2)
                    for t in range(T + 1):
                        for i in range(min(t + 1, T)):
                            last = nc.tensor.matmul(places(a.slot)[:, t, :],
                                                    before[:, :] if i == t else all_ones[:, :],
                                                    both[:, a.slot, i, :], start=(i == 0),
                                                    stop=(i == min(t, T - 1)))
                    last.then_inc(rank_ps, 1)
                a = at(2)
                if a:
                    pe.wait_ge(wide_done, a.index + 1)
                    since(pe, bc_done, a.index, 2, 2)
                    for n, (t0, t1) in enumerate(PARTS):
                        for t in range(t0, t1):
                            last = nc.tensor.matmul(ps[:, 4 + 2 * a.slot + n, (t - t0) * P:(t - t0 + 1) * P],
                                                    gate_w[:, a.slot, t, :], ident[:, :],
                                                    start=True, stop=True)
                        last.then_inc(bc_ps, 1)
            pipelined(pe, groups, 2, 2, 2, step)

        @block.scalar
        def _(act):
            def step(j, at):
                a = at(2)
                if a:
                    for n, (t0, t1) in enumerate(PARTS):
                        act.wait_ge(bc_ps, 2 * a.index + n + 1)
                        nc.scalar.activation(
                            gate_all[:, bass.ds(a.index * (T * P) + t0 * P, (t1 - t0) * P)],
                            ps[:, 4 + 2 * a.slot + n, 0:(t1 - t0) * P], ACT.Copy).then_inc(bc_done, 1)
                a = at(0)
                if a:
                    act.wait_ge(below_done, a.index + 1)
                    since(act, terms_done, a.index, 2)
                    since(act, total_done, a.index, 2)
                    nc.scalar.activation(prob[:, a.slot], below[:, a.slot], ACT.Exp)\
                        .then_inc(prob_done, 1)
            pipelined(act, groups, 2, 2, 2, step)

        @block.vector
        def _(dve):
            nc.vector.memset(carry[:, :], 0.0).then_inc(carry_set, 1)
            dve.wait_ge(carry_set, 1)

            def step(j, at):
                a = at(0)
                if a:
                    i, sl = a.index, a.slot
                    dve.wait_ge(l_ps, i + 1)
                    nc.vector.memset(held[:, :], 0.0)
                    for t in range(T):
                        last = nc.vector.max(top[:, sl, t, :], logits(sl)[:, t, :])
                    last.then_inc(top_done, 1)
                    dve.wait_ge(top_done, i + 1)
                    since(dve, prob_done, i, 2)
                    nc.vector.tensor_tensor(below[:, sl], logits(sl), each_expert(top[:, sl, :, 0]),
                                            ALU.subtract).then_inc(below_done, 1)
                    for t in range(T):
                        last = nc.vector.max_index(idx[:, sl, t, :], top[:, sl, t, :], logits(sl)[:, t, :])
                    last.then_inc(idx_done, 1)
                    dve.wait_ge(idx_done, i + 1)
                    nc.vector.tensor_copy(idf[:, sl], idx[:, sl, :, 0:2]).then_inc(idf_done, 1)
                    dve.wait_ge(idf_done, i + 1)
                    for n, out in enumerate((first, second)):
                        nc.vector.tensor_tensor(out[:, sl], each_tile(expert_ids[:, :]),
                                                each_expert(idf[:, sl, :, n]), ALU.is_equal)\
                            .then_inc(choice_done, 1)
                    dve.wait_ge(choice_done, 2 * i + 2)
                    since(dve, rank_ps, i, 2)
                    nc.vector.tensor_tensor(both[:, sl], first[:, sl], second[:, sl], ALU.add)\
                        .then_inc(both_done, 1)
                a = at(1)
                if a:
                    i, sl = a.index, a.slot
                    dve.wait_ge(rank_ps, i + 1)
                    since(dve, carry_done, i, 1)
                    nc.vector.tensor_tensor(count[:, sl], places(sl)[:, 0:T, :], each_tile(carry[:, :]),
                                            ALU.add).then_inc(count_done, 1)
                    dve.wait_ge(count_done, i + 1)
                    nc.vector.tensor_tensor(carry[:, :], places(sl)[:, T, :], carry[:, :], ALU.add)\
                        .then_inc(carry_done, 1)
                    nc.vector.scalar_tensor_tensor(out=kept[:, sl], in0=count[:, sl],
                                                   scalar=float(CAPACITY), in1=both[:, sl],
                                                   op0=ALU.is_lt, op1=ALU.mult).then_inc(kept_done, 1)
                    dve.wait_ge(kept_done, i + 1)
                    dve.wait_ge(prob_done, i + 1)
                    nc.vector.tensor_tensor(terms[:, sl], kept[:, sl], prob[:, sl], ALU.mult)\
                        .then_inc(terms_done, 1)
                    nc.vector.tensor_reduce(total[:, sl], prob[:, sl], AX.X, ALU.add)\
                        .then_inc(total_done, 1)
                    dve.wait_ge(terms_done, i + 1)
                    nc.vector.tensor_reduce(gsum[:, sl], terms[:, sl], AX.X, ALU.add)\
                        .then_inc(sum_done, 1)
                    dve.wait_ge(total_done, i + 1)
                    nc.vector.reciprocal(inv[:, sl], total[:, sl]).then_inc(inv_done, 1)
                    dve.wait_ge(sum_done, i + 1)
                    dve.wait_ge(inv_done, i + 1)
                    nc.vector.tensor_tensor(gate[:, sl], gsum[:, sl], inv[:, sl], ALU.mult)\
                        .then_inc(gate_done, 1)
                    dve.wait_ge(gate_done, i + 1)
                    since(dve, bc_ps, i, 2, 2)
                    nc.vector.tensor_copy(gate_w[:, sl], gate[:, sl].unsqueeze(2).to_broadcast([P, T, P]))\
                        .then_inc(wide_done, 1)
            pipelined(dve, groups, 2, 2, 2, step)


def shared_mlp(nc, tokens, h, xn, ps, w1, b1, w2, b2, gate_all):
    n = 416 if tokens % 832 == 0 else 260
    C = F0 // P
    ctx, sb, sem = stage_scope(nc)
    with ctx:
        g1 = sb("gelu_out", [P, 2, C, n])
        y = sb("mlp_gated", [P, 2, n])
        up_ps, g_done = sem("up_ps"), sem("gelu_done")
        y_ps, y_done, h_done = sem("down_ps"), sem("gated"), sem("h_added")
        block = ctx.enter_context(nc.Block())

        def since(eng, sm, index, lag):
            if not (isinstance(index, int) and index < lag):
                eng.wait_ge(sm, index - lag + 1)

        @block.tensor
        def _(pe):
            def step(j, at):
                a = at(0)
                if a:
                    for c in range(C):
                        if not (isinstance(a.index, int) and a.index < 1):
                            pe.wait_ge(g_done, C * a.index - C + c + 1)
                        nc.tensor.matmul(ps[:, c, 0:n], w1[:, c * P:(c + 1) * P],
                                         xn[:, bass.ds(a.index * n, n)], start=True, stop=True)\
                            .then_inc(up_ps, 1)
                a = at(1)
                if a:
                    pe.wait_ge(g_done, C * a.index + C)
                    since(pe, y_done, a.index, 2)
                    for c in range(C):
                        last = nc.tensor.matmul(ps[:, 4 + a.slot, 0:n], w2[:, c, :], g1[:, a.slot, c, :],
                                                start=(c == 0), stop=(c == C - 1))
                    last.then_inc(y_ps, 1)
            pipelined(pe, tokens // n, 2, 1, 2, step)

        @block.scalar
        def _(act):
            def step(j, at):
                a = at(0)
                if a:
                    since(act, y_ps, a.index, 2)
                    for c in range(C):
                        act.wait_ge(up_ps, C * a.index + c + 1)
                        nc.scalar.activation(g1[:, a.slot, c, :], ps[:, c, 0:n], ACT.Gelu,
                                             bias=b1[:, c:c + 1]).then_inc(g_done, 1)
            pipelined(act, tokens // n, 2, 1, 2, step)

        @block.vector
        def _(dve):
            def step(j, at):
                a = at(1)
                if a:
                    cols = bass.ds(a.index * n, n)
                    dve.wait_ge(y_ps, a.index + 1)
                    nc.vector.scalar_tensor_tensor(out=y[:, a.slot, :], in0=ps[:, 4 + a.slot, 0:n],
                                                   scalar=b2[:, 0:1], in1=gate_all[:, cols],
                                                   op0=ALU.add, op1=ALU.mult).then_inc(y_done, 1)
                    dve.wait_ge(y_done, a.index + 1)
                    nc.vector.tensor_tensor(h[:, cols], h[:, cols], y[:, a.slot, :], ALU.add)\
                        .then_inc(h_done, 1)
            pipelined(dve, tokens // n, 2, 1, 2, step)


def dense_mixture(nc, tokens, h, xn, ps, ident, gate_w, gate_b, expert_ids, w1, b1, w2, b2, out):
    n = P if tokens % P == 0 else 104
    SL = 2
    C = F1 // P * E1
    HB = 4
    ctx, sb, sem = stage_scope(nc)
    with ctx:
        xs = sb("xn_tile_m", [P, SL, n])
        held = sb("held_m", [P, 1])
        hs = sb("h_tile_m", [P, SL, n])
        logit = sb("logit_m", [P, SL, E1])
        top = sb("top8_m", [P, SL, 8])
        idx = sb("index8_m", [P, SL, 8], U32)
        idf = sb("index_m", [P, SL, 2])
        gap = sb("gap_m", [P, SL, 1])
        eg = sb("exp_gap_m", [P, SL, 1])
        ws = sb("weight_sum_m", [P, SL, 1])
        wa = sb("weight_first_m", [P, SL, 1])
        wb = sb("weight_second_m", [P, SL, 1])
        first = sb("first_weight_m", [P, SL, E1])
        wt = sb("weights_m", [P, SL, E1])
        wtt = sb("weightsT_m", [E1, SL, n])
        hid = sb("hidden_m", [P, SL, C, n])
        acc = sb("acc_m", [P, SL, D])
        copied, l_ps = sem("copied_m"), sem("logits_ps_m")
        dstep = sem("weight_steps_m")
        gap_done, eg_done, wt_done = sem("gap_done_m"), sem("eg_done_m"), sem("wt_done_m")
        wtt_ps, wtt_sb = sem("wT_ps_m"), sem("wT_sb_m")
        base_ps, base_sb = sem("base_ps_m"), sem("base_sb_m")
        hid_ps, hid_sb = sem("hid_ps_m"), sem("hid_sb_m")
        y_ps, acc_done = sem("y_ps_m"), sem("acc_done_m")
        stored = [sem(f"stored_m{i}") for i in range(SL)]
        block = ctx.enter_context(nc.Block())
        NB = C // HB
        D_ = 2
        STEPS = 8

        def since(eng, sm, index, lag, per=1):
            if not (isinstance(index, int) and index < lag):
                eng.wait_ge(sm, index * per - (lag - 1) * per)

        def base_bank(slot):
            return ps[0:n, 4 + slot, 0:D]

        def wtt_bank(slot):
            return ps[0:E1, 7, 0:n]

        @block.sync
        def _(sp):
            def step(j, at):
                a = at(2)
                if a:
                    sp.wait_ge(acc_done, E1 * a.index + E1)
                    sp.dma_start(out[bass.ds(a.index * n, n), :], acc[0:n, a.slot, :])\
                        .then_inc(stored[a.slot], 16)
            pipelined(sp, tokens // n, SL, D_, SL, step)
            for i in range(SL):
                sp.wait_ge(stored[i], 16 * len(range(i, tokens // n, SL)))

        @block.gpsimd
        def _(pool):
            def step(j, at):
                a = at(0)
                if a:
                    since(pool, l_ps, a.index, SL)
                    since(pool, base_ps, a.index, SL)
                    cols = bass.ds(a.index * n, n)
                    nc.gpsimd.tensor_copy(xs[:, a.slot, :], xn[:, cols])
                    nc.gpsimd.tensor_copy(hs[:, a.slot, :], h[:, cols]).then_inc(copied, 1)
            pipelined(pool, tokens // n, SL, D_, SL, step)

        @block.tensor
        def _(pe):
            def up(a, b):
                if b >= 2:
                    pe.wait_ge(hid_sb, NB * a.index + b - 1)
                elif not (isinstance(a.index, int) and a.index < 1):
                    pe.wait_ge(hid_sb, NB * a.index + b - 1)
                for i in range(HB):
                    c = b * HB + i
                    last = nc.tensor.matmul(ps[:, b % 2, i * P:i * P + n], w1[:, c * P:(c + 1) * P],
                                            xn[:, bass.ds(a.index * n, n)], start=True, stop=True)
                last.then_inc(hid_ps, 1)

            def down(a, b):
                pe.wait_ge(hid_sb, NB * a.index + (b + 1) * (NB // 2))
                if not (isinstance(a.index, int) and a.index < 1):
                    pe.wait_ge(acc_done, E1 * a.index - E1 + (b + 1) * (E1 // 2))
                for e in range(b * E1 // 2, (b + 1) * E1 // 2):
                    for f in range(F1 // P):
                        c = e * (F1 // P) + f
                        last = nc.tensor.matmul(ps[0:n, 2 + b, (e % 4) * D:(e % 4 + 1) * D],
                                                hid[:, a.slot, c, :], w2[:, c, :],
                                                start=(f == 0), stop=(f == F1 // P - 1))
                last.then_inc(y_ps, 1)

            def step(j, at):
                a = at(0)
                if a:
                    pe.wait_ge(copied, a.index + 1)
                    since(pe, dstep, a.index, 1, STEPS)
                    nc.tensor.matmul(ps[0:n, 6, 0:E1], xs[:, a.slot, :],
                                     gate_w[:, :], start=True, stop=True).then_inc(l_ps, 1)
                    up(a, 0)
                b = at(1)
                if b:
                    pe.wait_ge(wt_done, b.index + 1)
                    since(pe, wtt_sb, b.index, 1)
                    nc.tensor.transpose(wtt_bank(b.slot), wt[0:n, b.slot, :], ident[0:n, 0:n])\
                        .then_inc(wtt_ps, 1)
                    down(b, 0)
                if a:
                    up(a, 1)
                if b:
                    pe.wait_ge(wtt_sb, b.index + 1)
                    since(pe, base_sb, b.index, SL)
                    nc.tensor.matmul(base_bank(b.slot), hs[:, b.slot, :], ident[:, :],
                                     start=True, stop=False)
                    nc.tensor.matmul(base_bank(b.slot), wtt[:, b.slot, :], b2[0:E1, :],
                                     start=False, stop=True).then_inc(base_ps, 1)
                if a:
                    up(a, 2)
                if b:
                    down(b, 1)
                if a:
                    up(a, 3)
            pipelined(pe, tokens // n, SL, D_, SL, step)

        @block.scalar
        def _(act):
            def relu(a, b):
                act.wait_ge(hid_ps, NB * a.index + b + 1)
                if b == 0:
                    since(act, y_ps, a.index, SL, 2)
                for i in range(HB):
                    c = b * HB + i
                    last = nc.scalar.activation(hid[:, a.slot, c, :], ps[:, b % 2, i * P:i * P + n],
                                                ACT.Relu, bias=b1[:, c:c + 1])
                last.then_inc(hid_sb, 1)

            def step(j, at):
                a, b = at(0), at(1)
                if a:
                    relu(a, 0)
                    act.wait_ge(gap_done, a.index + 1)
                    nc.scalar.activation(eg[0:n, a.slot, :], gap[0:n, a.slot, :], ACT.Exp)\
                        .then_inc(eg_done, 1)
                if b:
                    act.wait_ge(wtt_ps, b.index + 1)
                    since(act, base_ps, b.index, SL)
                    nc.scalar.activation(wtt[:, b.slot, :], wtt_bank(b.slot), ACT.Copy)\
                        .then_inc(wtt_sb, 1)
                if a:
                    relu(a, 1)
                if b:
                    act.wait_ge(base_ps, b.index + 1)
                    if not (isinstance(b.index, int) and b.index < SL):
                        act.wait_ge(stored[b.slot], (b.index - b.slot) * (16 // SL))
                    nc.scalar.activation(acc[0:n, b.slot, :], base_bank(b.slot), ACT.Copy)\
                        .then_inc(base_sb, 1)
                if a:
                    relu(a, 2)
                    relu(a, 3)
            pipelined(act, tokens // n, SL, D_, SL, step)

        @block.vector
        def _(dve):
            def step(j, at):
                a = at(0)
                if a:
                    i, sl = a.index, a.slot
                    done = [0]

                    def chained(ins):
                        done[0] += 1
                        ins.then_inc(dstep, 1)
                        dve.wait_ge(dstep, STEPS * i + done[0])

                    dve.wait_ge(l_ps, i + 1)
                    chained(nc.vector.tensor_tensor(logit[0:n, sl, :],
                                                    ps[0:n, 6, 0:E1],
                                                    gate_b[0:n, :], ALU.add))
                    nc.vector.memset(held[:, :], 0.0)
                    chained(nc.vector.max(top[0:n, sl, :], logit[0:n, sl, :]))
                    since(dve, eg_done, i, SL)
                    nc.vector.tensor_tensor(gap[0:n, sl, :], top[0:n, sl, 1:2], top[0:n, sl, 0:1],
                                            ALU.subtract).then_inc(gap_done, 1)
                    chained(nc.vector.max_index(idx[0:n, sl, :], top[0:n, sl, :], logit[0:n, sl, :]))
                    chained(nc.vector.tensor_copy(idf[0:n, sl, :], idx[0:n, sl, 0:2]))
                    dve.wait_ge(eg_done, i + 1)
                    chained(nc.vector.tensor_scalar(ws[0:n, sl, :], eg[0:n, sl, :], 1.0, None, ALU.add))
                    chained(nc.vector.reciprocal(wa[0:n, sl, :], ws[0:n, sl, :]))
                    nc.vector.tensor_scalar(first[0:n, sl, :], expert_ids[0:n, 0:E1], idf[0:n, sl, 0:1],
                                            wa[0:n, sl, :], ALU.is_equal, ALU.mult)
                    chained(nc.vector.tensor_tensor(wb[0:n, sl, :], eg[0:n, sl, :], wa[0:n, sl, :],
                                                    ALU.mult))
                    since(dve, wtt_ps, i, SL)
                    chained(nc.vector.tensor_scalar(wt[0:n, sl, :], expert_ids[0:n, 0:E1],
                                                    idf[0:n, sl, 1:2], wb[0:n, sl, :],
                                                    ALU.is_equal, ALU.mult))
                    nc.vector.tensor_tensor(wt[0:n, sl, :], wt[0:n, sl, :], first[0:n, sl, :],
                                            ALU.add).then_inc(wt_done, 1)
                    assert done[0] == STEPS
                a = at(1)
                if a:
                    i, sl = a.index, a.slot
                    dve.wait_ge(wt_done, i + 1)
                    dve.wait_ge(base_sb, i + 1)
                    for e in range(E1):
                        if e % 4 == 0:
                            dve.wait_ge(y_ps, 2 * i + e // 4 + 1)
                        if e:
                            dve.wait_ge(acc_done, E1 * i + e)
                        nc.vector.scalar_tensor_tensor(
                            out=acc[0:n, sl, :], in0=ps[0:n, 2 + e // 4, (e % 4) * D:(e % 4 + 1) * D],
                            scalar=wt[0:n, sl, e:e + 1], in1=acc[0:n, sl, :],
                            op0=ALU.mult, op1=ALU.add).then_inc(acc_done, 1)
            pipelined(dve, tokens // n, SL, D_, SL, step)


def fold_weights(nc, ps, mean_w, spread_w, alphas_raw, alphas, bv_col, alpha_col_raw, w_out, b_out, b_out_all,
                 wt_t, w_out2, w_dist):
    ctx, sb, sem = stage_scope(nc)
    with ctx:
        acol = sb("alpha_col", [P, CH, ORDER])
        asum = sb("alpha_sum", [P, CH])
        abv = sb("alpha_bv", [P, CH])
        gelu_done, asum_done, abv_done = sem("alphas_gelu"), sem("alpha_summed"), sem("alpha_bv_done")
        folded_ps, folded = sem("folded_ps"), sem("folded")
        block = ctx.enter_context(nc.Block())

        @block.scalar
        def _(act):
            nc.scalar.activation(acol[:, :, :], alpha_col_raw, ACT.Gelu).then_inc(gelu_done, 1)
            nc.scalar.activation(alphas[:, :, :], alphas_raw, ACT.Gelu).then_inc(gelu_done, 1)
            act.wait_ge(gelu_done, 2)

        @block.tensor
        def _(pe):
            for c in range(CH):
                last = nc.tensor.matmul(ps[:, 0, 0:D], wt_t[:, c, :], w_out2[:, c, :],
                                        start=(c == 0), stop=(c == CH - 1))
            pe.wait_ge(abv_done, 1)
            for c in range(CH):
                last = nc.tensor.matmul(ps[:, 1, 0:1], w_out[:, c, :], abv[:, c:c + 1],
                                        start=(c == 0), stop=(c == CH - 1))
            last.then_inc(folded_ps, 1)

        @block.vector
        def _(dve):
            nc.vector.memset(mean_w[:, :], 1.0 / D).then_inc(folded, 1)
            dve.wait_ge(gelu_done, 2)
            nc.vector.tensor_reduce(asum[:, :], acol[:, :, :], AX.X, ALU.add).then_inc(asum_done, 1)
            dve.wait_ge(asum_done, 1)
            nc.vector.tensor_tensor(abv[:, :], asum[:, :], bv_col, ALU.mult).then_inc(abv_done, 1)
            dve.wait_ge(folded_ps, 1)
            nc.vector.tensor_copy(w_dist[:, :], ps[:, 0, 0:D]).then_inc(folded, 1)
            nc.vector.tensor_tensor(b_out_all[:, :], ps[:, 1, 0:1], b_out, ALU.add).then_inc(folded, 1)
            nc.vector.memset(spread_w[:, :], 1.0 / 32).then_inc(folded, 1)
            dve.wait_ge(folded, 4)


def vit_tower(nc, A, images, out):
    tokens = images * SEQ
    ctx = ExitStack()
    with ctx:
        ps = ctx.enter_context(nc.psum_tensor("ps", [P, 8, BANK], FP32))
        S = {}
        own = ("w_tok", "b_tok", "pos", "cls")
        own_loads, later_loads = [], []
        for name, (ap, shape) in A.items():
            if name in ("x_main", "x_tail"):
                continue
            S[name] = ctx.enter_context(nc.sbuf_tensor(f"s_{name}", shape,
                                                       BF16 if name in ("before", "all_ones") else FP32))
            (own_loads if name in own else later_loads).append((S[name][tuple(slice(None) for _ in shape)], ap))
        h = ctx.enter_context(nc.sbuf_tensor("h", [P, tokens], FP32))
        xn = ctx.enter_context(nc.sbuf_tensor("xn", [P, tokens], FP32))
        mean_w = ctx.enter_context(nc.sbuf_tensor("mean_w", [P, P], FP32))
        spread_w = ctx.enter_context(nc.sbuf_tensor("spread_w", [P, P], FP32))
        w_dist = ctx.enter_context(nc.sbuf_tensor("w_dist", [P, D], FP32))

        patch_embed(nc, images, A["x_main"][0], A["x_tail"][0], h, ps, S["w_tok"], S["b_tok"],
                    S["pos"], S["cls"], own_loads, later_loads)
        alphas = ctx.enter_context(nc.sbuf_tensor("alphas", [SEQ, ORDER, H], FP32))
        b_out0 = ctx.enter_context(nc.sbuf_tensor("b_out0", [P, 1], FP32))
        fold_weights(nc, ps, mean_w, spread_w, S["a0_alphas"][:, :, :], alphas, S["a0_bv"][:, :],
                     S["a0_alpha_col"][:, :, :], S["a0_wout"], S["a0_bout"][:, :], b_out0,
                     S["a1_wt_t"], S["a1_wout2"], w_dist)
        layer_norm(nc, "a0", tokens, h, xn, ps, mean_w, spread_w)
        attention(nc, "a0", images, h, xn, ps, S["ident"], S["a0_wqkv"], S["a0_wout"], b_out0,
                  ORDER, b_qk=S["a0_bqk"], alphas=alphas)
        layer_norm(nc, "f0", tokens, h, xn, ps, mean_w, spread_w)
        with nc.sbuf_tensor("gate_all", [P, tokens], FP32) as gate_all:
            route_with_capacity(nc, tokens, xn, ps, S["f0_router"], S["expert_ids"], S["before"],
                                S["all_ones"], S["ident"], gate_all)
            shared_mlp(nc, tokens, h, xn, ps, S["f0_w1"], S["f0_b1"], S["f0_w2"], S["f0_b2"], gate_all)
        layer_norm(nc, "a1", tokens, h, xn, ps, mean_w, spread_w)
        attention(nc, "a1", images, h, xn, ps, S["ident"], S["a1_wqkv"], S["a1_wout"], S["a1_bout"],
                  1, w_dist=w_dist, dist=S["dist"])
        layer_norm(nc, "f1", tokens, h, xn, ps, mean_w, spread_w)
        dense_mixture(nc, tokens, h, xn, ps, S["ident"], S["f1_gate"], S["f1_gate_b"], S["expert_ids"],
                      S["f1_w1"], S["f1_b1"], S["f1_w2"], S["f1_b2"], out)


def kernel(x, L0_tok_W, L0_tok_b, L0_tok_class_token, L0_tok_pos_embed, L0_attn_Wqkv, L0_attn_bqkv,
           L0_attn_Wout, L0_attn_bout, L0_attn_alphas_raw, L0_ffn_router_w, L0_ffn_w1, L0_ffn_b1,
           L0_ffn_w2, L0_ffn_b2, L1_attn_W_qkv, L1_attn_W_out, L1_attn_b_out, L1_ffn_gate_w,
           L1_ffn_gate_b, L1_ffn_w1, L1_ffn_b1, L1_ffn_w2, L1_ffn_b2):
    import math
    import numpy as np
    import ml_dtypes
    import concourse.bacc as bacc
    from concourse.bass_utils import run_bass_kernel_spmd

    a = np.asarray
    images = x.shape[0]
    chunks = images // CHUNK_IMAGES
    n = CHUNK_IMAGES * PATCHES

    def patch_rows(x):
        t = a(x).reshape(chunks, CHUNK_IMAGES, 3, GRID, PATCH, GRID, PATCH)
        return t.transpose(0, 2, 4, 6, 1, 3, 5).reshape(chunks, IN_D, n)
    rows = patch_rows(x)
    w_tok_t = a(L0_tok_W).T
    w_tok = np.zeros((P, KT + 1, D), np.float32)
    w_tok[:, :KT] = w_tok_t[:KT * P].reshape(KT, P, D).transpose(1, 0, 2)
    w_tok[:KR, KT] = w_tok_t[KT * P:]

    def chunk_rows(w):
        return w.reshape(-1, P, w.shape[-1]).transpose(1, 0, 2)

    def repeated(v, rows):
        return np.broadcast_to(a(v)[None], (rows,) + a(v).shape)

    wqkv1 = a(L1_attn_W_qkv)
    wout1 = a(L1_attn_W_out).reshape(H, 2, DH, D)
    place = np.arange(1, SEQ + 1, dtype=np.float32)
    dist = np.exp(-np.abs(place[None, :] - place[:, None]) / np.float32(math.e))
    dist = (dist / dist.sum(-1)).T
    rank = np.arange(P)
    data = {
        "x_main": rows[:, :KT * P].reshape(chunks, KT, P, n).transpose(0, 2, 1, 3),
        "x_tail": rows[:, KT * P:],
        "w_tok": w_tok,
        "b_tok": a(L0_tok_b)[:, None],
        "pos": a(L0_tok_pos_embed).T,
        "cls": a(L0_tok_class_token).T,
        "a0_wqkv": a(L0_attn_Wqkv),
        "a0_bqk": a(L0_attn_bqkv)[:2 * INNER].reshape(2 * CH, P).T,
        "a0_bv": a(L0_attn_bqkv)[2 * INNER:].reshape(CH, P).T,
        "a0_alpha_col": np.repeat(a(L0_attn_alphas_raw).T, DH, axis=0).reshape(CH, P, ORDER)
        .transpose(1, 0, 2),
        "a0_wout": chunk_rows(a(L0_attn_Wout)),
        "a0_bout": a(L0_attn_bout)[:, None],
        "a0_alphas": repeated(L0_attn_alphas_raw, SEQ),
        "f0_router": a(L0_ffn_router_w).T,
        "f0_w1": a(L0_ffn_w1).T,
        "f0_b1": a(L0_ffn_b1).reshape(F0 // P, P).T,
        "f0_w2": chunk_rows(a(L0_ffn_w2).T),
        "f0_b2": a(L0_ffn_b2)[:, None],
        "a1_wqkv": wqkv1[:, :3 * INNER],
        "a1_wt_t": chunk_rows(wqkv1[:, 3 * INNER:].T),
        "a1_wout": chunk_rows(wout1[:, 0].reshape(INNER, D)),
        "a1_wout2": chunk_rows(wout1[:, 1].reshape(INNER, D)),
        "a1_bout": a(L1_attn_b_out)[:, None],
        "f1_gate": a(L1_ffn_gate_w),
        "f1_gate_b": repeated(L1_ffn_gate_b, P),
        "f1_w1": a(L1_ffn_w1).transpose(1, 0, 2).reshape(D, E1 * F1),
        "f1_b1": a(L1_ffn_b1).reshape(E1 * F1 // P, P).T,
        "f1_w2": chunk_rows(a(L1_ffn_w2).reshape(E1 * F1, D)),
        "f1_b2": a(L1_ffn_b2),
        "ident": np.eye(P, dtype=np.float32),
        "dist": dist.astype(np.float32),
        "expert_ids": np.tile(np.arange(E0, dtype=np.float32), (P, 1)),
        "before": (rank[:, None] < rank[None, :]).astype(ml_dtypes.bfloat16),
        "all_ones": np.ones((P, P), ml_dtypes.bfloat16),
    }
    nc = bacc.Bacc("TRN2", target_bir_lowering=False, num_devices=1)
    arrays, A = {}, {}
    for name, v in data.items():
        v = np.ascontiguousarray(v)
        arrays[f"in_{name}"] = v
        ap = nc.dram_tensor(f"in_{name}", v.shape, mybir.dt.from_np(v.dtype), kind="ExternalInput").ap()
        A[name] = (ap, list(v.shape))
    out = nc.dram_tensor("out", (images * SEQ, D), FP32, kind="ExternalOutput").ap()
    vit_tower(nc, A, images, out)
    r = run_bass_kernel_spmd(nc, [arrays], core_ids=[0])
    return r.results[0]["out"].reshape(images, SEQ, D)
```
